# Optimizing a Trainium2 kernel written in Bass

```python
import numpy as np
import jax
import jax.numpy as jnp

def _softmax(x, axis=-1):
    return jax.nn.softmax(x, axis=axis)

def _gelu(x):
    return jax.nn.gelu(x, approximate=True)

def _silu(x):
    return jax.nn.silu(x)

def _sigmoid(x):
    return jax.nn.sigmoid(x)

def _layernorm(x, axis=-1, eps=1e-05):
    m = jnp.mean(x, axis=axis, keepdims=True)
    v = jnp.var(x, axis=axis, keepdims=True)
    return (x - m) / jnp.sqrt(v + eps)

def _scatter_add(tgt, idx, src, axis=0):
    return tgt.at[idx].add(src)

def _segment_sum(src, seg, n):
    return jax.ops.segment_sum(src, seg, n)
kernel_name = 'mk_adj_preln_d1_adj_r2_0b76ef'

def setup_inputs(seed: int=0):
    np.random.seed(seed)
    _w = jnp.asarray

    def _rec_inputs():
        import jax
        import jax.numpy as jnp
        _gk = jax.random.key(seed)
        x = -0.0005207 + 1.001 * jax.random.normal(jax.random.fold_in(_gk, 1), (4096, 128), jnp.float32)
        _w = (1.0 + jnp.arange(4096, dtype=jnp.float32)) ** (-0.5)
        _w = _w / _w.mean()
        _pij = jnp.clip(0.00195312 * _w[:, None] * _w[None, :], 0.0, 1.0)
        _a = jax.random.uniform(jax.random.fold_in(_gk, 2), (4096, 4096)) < _pij
        adj = _a.astype(jnp.int32)
        return (x, adj)
    x, adj = _rec_inputs()

    def _L0_gnn_setup():
        import jax, jax.numpy as jnp
        import numpy as np
        N, IN_DIM, OUT_DIM = (4096, 128, 128)
        NEG_INF = -1000000000.0
        key = jax.random.key(seed)
        k1, k2, k3, k4 = jax.random.split(key, 4)
        X = jax.random.normal(k1, (N, IN_DIM), dtype=jnp.float32)
        A = jax.random.randint(k2, (N, N), 0, 2).astype(jnp.int32)
        W_fc = jax.random.normal(k3, (IN_DIM, OUT_DIM), dtype=jnp.float32) * (1.0 / np.sqrt(IN_DIM))
        b_fc = jnp.zeros((OUT_DIM,), dtype=jnp.float32)
        w_att = jax.random.normal(k4, (2 * OUT_DIM,), dtype=jnp.float32) * (1.0 / np.sqrt(2 * OUT_DIM))
        b_att = jnp.zeros((), dtype=jnp.float32)
        return {'X': X, 'A': A, 'W_fc': W_fc, 'b_fc': b_fc, 'w_att': w_att, 'b_att': b_att}
    _L0_gnn_all = _L0_gnn_setup()
    _L0_gnn_in = {k: v for k, v in _L0_gnn_all.items() if k in ('W_fc', 'b_fc', 'w_att', 'b_att')}
    del _L0_gnn_all
    return {'x': x, 'adj': adj, 'L0_gnn_W_fc': _L0_gnn_in['W_fc'], 'L0_gnn_b_fc': _L0_gnn_in['b_fc'], 'L0_gnn_w_att': _L0_gnn_in['w_att'], 'L0_gnn_b_att': _L0_gnn_in['b_att']}

def reference(x, adj, L0_gnn_W_fc, L0_gnn_b_fc, L0_gnn_w_att, L0_gnn_b_att):
    import jax
    import jax.numpy as jnp

    def _L0_gnn_ref(X, A, W_fc, b_fc, w_att, b_att):
        import jax, jax.numpy as jnp
        import numpy as np
        N, IN_DIM, OUT_DIM = (4096, 128, 128)
        NEG_INF = -1000000000.0
        H = X @ W_fc + b_fc
        d = H.shape[1]
        s_src = H @ w_att[:d]
        s_dst = H @ w_att[d:]
        scores = s_src[:, None] + s_dst[None, :] + b_att
        scores = jnp.where(A > 0, scores, jnp.float32(NEG_INF))
        alpha = jax.nn.softmax(scores, axis=1)
        return alpha @ H
    h = jnp.maximum(_layernorm(x, axis=-1), 0.0)
    x = x + _L0_gnn_ref(h, adj, L0_gnn_W_fc, L0_gnn_b_fc, L0_gnn_w_att, L0_gnn_b_att)
    return x

_drawn_inputs = setup_inputs


def setup_inputs(seed=0):
    import zlib

    import numpy as np

    out = dict(_drawn_inputs(seed))
    spreads = {'L0_gnn_b_fc': (0.0, 0.1)}
    factors = {}
    for name, (base, spread) in spreads.items():
        noise = np.random.default_rng([zlib.crc32(name.encode()), seed]).standard_normal(out[name].shape)
        drawn = base * np.exp(spread * noise) if base else spread * noise
        out[name] = jnp.asarray(drawn.astype(out[name].dtype))
    for name, factor in factors.items():
        out[name] = (out[name] * factor).astype(out[name].dtype)
    return out
```

```python
from contextlib import ExitStack

import concourse.bass as bass
from concourse import mybir

P = 128
ALU = mybir.AluOpType
ACT = mybir.ActivationFunctionType
BF16 = mybir.dt.bfloat16
F32 = mybir.dt.float32
I32 = mybir.dt.int32
AX_X = mybir.AxisListType.X
RMAX = bass.bass_isa.ReduceOp.max
RADD = bass.bass_isa.ReduceOp.add

SUB = 4
NEG_INF = -1.0e9
EPS = 1.0e-5
MAX_SPREAD = 40.0
LOWEST_SCORE = -9.0e8


def gnn_kernel(nc, x, adj_t, adj, w_fc, w_fc_t, b_fc, w_att, a_att, b_att, out):
    N, D = x.shape
    T = N // P
    GROUPS, CHUNKS = adj_t.shape[0], adj_t.shape[1]
    Q = T // CHUNKS
    GW = SUB * P
    XP = T // Q
    E = D + 2
    GC = 3 * D + 3
    assert D == P and GROUPS * SUB == T and XP == CHUNKS

    with ExitStack() as ctx:
        def sb(name, shape, dt):
            return ctx.enter_context(nc.sbuf_tensor(name, shape, dt))

        def sem(name):
            return ctx.enter_context(nc.semaphore(name))

        adj_int = sb("adj_int", [P, CHUNKS, Q, GW], I32)
        mask = sb("mask", [P, CHUNKS, Q, GW], BF16)
        G = sb("G", [P, T, GC + 1], BF16)
        xs = sb("xs", [P, T, D], F32)
        HS = sb("HS", [P, T, E], F32)
        xc = sb("xc", [P, 2, Q, D], F32)
        hT = sb("hT", [P, 2, Q, P], F32)
        rest = sb("rest", [P, 2, Q, D], F32)
        evac = sb("evac", [P, SUB, GC], F32)
        num = sb("num", [P, SUB, D], F32)
        w_ext = sb("w_ext", [P, E], F32)
        w_t = sb("w_t", [P, D], F32)
        a_sb = sb("a_sb", [P, 2], F32)
        b_row = sb("b_row", [P, D], F32)
        ident = sb("ident", [P, P], F32)
        neg1 = sb("neg1", [1, P], F32)
        sumH = sb("sumH", [P, D], F32)
        partH = sb("partH", [P, D], F32)
        stats = sb("stats", [P, T, 6], F32)
        sum2 = sb("sum2", [P, T], F32)
        dm = sb("dm", [P, T], F32)
        var = sb("var", [P, T], F32)
        rstd = sb("rstd", [P, T], F32)
        expo = sb("expo", [P, T], F32)
        d0 = sb("d0", [P, T], F32)
        wt = sb("wt", [P, T], F32)
        wrest = sb("wrest", [P, T], F32)
        wr = sb("wr", [P, T], F32)
        dmx = sb("dmx", [P, 1], F32)
        dtop = sb("dtop", [1, 1], F32)
        negD = sb("negD", [P, 1], F32)
        den = sb("den", [P, SUB], F32)
        emp = sb("emp", [P, SUB], F32)
        rden = sb("rden", [P, SUB], F32)

        sneg = sb("sneg", [P, 2], F32)
        snegr = sb("snegr", [P, 2], F32)
        a_row = sb("a_row", [P, 2, D], F32)
        ab = sb("ab", [P, 2, D], F32)
        ba = sb("ba", [P, 2], F32)
        batt = sb("batt", [P, 1], F32)
        s_full = sb("s_full", [P, T], F32)
        low = sb("low", [P, 2], F32)
        flag = sb("flag", [P, 1], I32)
        wide = adj_int[:].rearrange("p c q n -> p (c q n)").rearrange("p (b j) -> p b j", b=4)
        gen_adj = wide[:, 0, :]
        gen_d = wide[:, 1, :].bitcast(F32)
        gen_s = wide[:, 2, :].bitcast(F32)
        gen_p = wide[:, 3, :].bitcast(F32)
        gen_H = mask[:].rearrange("p c q n -> p (c q n)").bitcast(F32)[:, 0:T * D].rearrange("p (t d) -> p t d", t=T)
        d_full = sb("d_full", [P, T], F32)
        gen_x = sb("gen_x", [P, D], F32)
        gen_nmax = sb("gen_nmax", [P, 1], F32)
        gen_den = sb("gen_den", [P, 1], F32)
        gen_rden = sb("gen_rden", [P, 1], F32)
        d_line = nc.dram_tensor("d_line", [P, T], F32)

        bank = ctx.enter_context(nc.psum_tensor("bank", [P, 8, 512], F32))
        ps_T = [bank[:, i, :] for i in range(2)]
        ps_H = [bank[:, 2 + 2 * i:4 + 2 * i, 0:2 * E] for i in range(2)]
        ps_gen = bank[:, 2, 0:D]
        ps_wa = bank[:, 6, 0:2]
        ps_dmx = bank[0:1, 6, 128:256]
        ps_negD = bank[:, 7, 0:1]

        s_w = sem("s_w")
        s_b = sem("s_b")
        s_x = [sem(f"s_x{k}") for k in range(XP)]
        s_adj = [sem(f"s_adj{c}") for c in range(CHUNKS)]
        s_id0 = sem("s_id0")
        s_id = sem("s_id")
        s_wa = sem("s_wa")
        s_wext = sem("s_wext")
        s_dve = sem("s_dve")
        s_stats = sem("s_stats")
        s_xc = sem("s_xc")
        s_T = sem("s_T")
        s_hT = sem("s_hT")
        s_H = sem("s_H")
        s_HS = sem("s_HS")
        s_var = sem("s_var")
        s_rstd = sem("s_rstd")
        s_dmx = sem("s_dmx")
        s_dmxT = sem("s_dmxT")
        s_dtop = sem("s_dtop")
        s_psD = sem("s_psD")
        s_negD = sem("s_negD")
        s_wt = sem("s_wt")
        s_wr = sem("s_wr")
        s_wparts = sem("s_wparts")
        s_g1 = sem("s_g1")
        s_rest = sem("s_rest")
        s_g2 = sem("s_g2")
        s_g3 = sem("s_g3")
        s_mask = sem("s_mask")
        s_chunk = sem("s_chunk")
        s_evac = sem("s_evac")
        s_comb = sem("s_comb")
        s_res = sem("s_res")
        s_partH = sem("s_partH")
        s_sumH = sem("s_sumH")
        s_pool = sem("s_pool")
        s_xb = sem("s_xb")
        s_out = sem("s_out")

        s_ab = sem("s_ab")
        s_sneg = sem("s_sneg")
        s_snegr = sem("s_snegr")
        s_flag = sem("s_flag")
        g_d = sem("g_d")
        g_dline = sem("g_dline")
        g_dB = sem("g_dB")
        g_row = sem("g_row")
        g_read = sem("g_read")
        g_dve = sem("g_dve")
        g_score = sem("g_score")
        g_prob = sem("g_prob")
        g_T = sem("g_T")
        g_pT = sem("g_pT")
        g_mm = sem("g_mm")
        g_res = sem("g_res")
        g_out = sem("g_out")

        x_v = x.rearrange("(p t) d -> p t d", p=P)
        out_v = out.rearrange("(p t) d -> p t d", p=P)
        adj_v = adj.rearrange("(p t) j -> p t j", p=P)

        block = ctx.enter_context(nc.Block())

        @block.sync
        def _(sp):
            for k in range(XP):
                sp.dma_start(xs[:, k * Q:(k + 1) * Q, :], x_v[:, k * Q:(k + 1) * Q, :]).then_inc(s_x[k], 16)
                if k == 0:
                    sp.dma_start(w_t[:], w_fc_t).then_inc(s_w, 16)
                    sp.dma_start(a_sb[:], a_att).then_inc(s_w, 16)
                    sp.dma_start(w_ext[:, 0:D], w_fc).then_inc(s_w, 16)
            sp.dma_start(b_row[:], b_fc.partition_broadcast(P)).then_inc(s_b, 16)
            sp.dma_start(a_row[:].rearrange("p c d -> p (c d)"), w_att.partition_broadcast(P)).then_inc(s_ab, 16)
            sp.dma_start(batt[:], b_att.partition_broadcast(P)).then_inc(s_ab, 16)
            for c in range(CHUNKS):
                sp.dma_start(adj_int[:, c], adj_t[0, c]).then_inc(s_adj[c], 16)
            with sp.Fori(1, GROUPS) as g:
                for c in range(CHUNKS):
                    sp.wait_ge(s_mask, (g - 1) * CHUNKS + c + 1)
                    sp.dma_start(adj_int[:, c], adj_t[bass.ds(g, 1), c].rearrange("o p q n -> (o p) q n")).then_inc(s_adj[c], 16)
            sp.wait_ge(s_flag, 1)
            general = sp.value_load(flag[0:1, 0:1], min_val=0, max_val=1)
            with sp.If(general != 0):
                sp.wait_ge(g_d, 1)
                sp.dma_start(d_line.ap(), d_full[:]).then_inc(g_dline, 16)
                sp.wait_ge(g_dline, 16)
                sp.dma_start(gen_d, d_line.ap().rearrange("p t -> (p t)").partition_broadcast(P)).then_inc(g_dB, 16)
                sp.wait_ge(s_out, 16 * GROUPS)
                with sp.Fori(0, T) as s:
                    sp.wait_ge(g_read, s + 1)
                    sp.dma_start(gen_adj, adj_v[:, bass.ds(s, 1), :].rearrange("p o j -> p (o j)")).then_inc(g_row, 16)
                    sp.dma_start(gen_x[:], x_v[:, bass.ds(s, 1), :].rearrange("p o d -> p (o d)")).then_inc(g_row, 16)
                    sp.wait_ge(g_res, s + 1)
                    sp.dma_start(out_v[:, bass.ds(s, 1), :].rearrange("p o d -> p (o d)"), gen_x[:]).then_inc(g_out, 16)
                    sp.wait_ge(g_out, s * 16 + 16)
                    sp.sem_inc(g_read, 1)
            sp.end_ifs()

        @block.gpsimd
        def _(pool):
            nc.gpsimd.memset(expo[:], -0.5)
            nc.gpsimd.memset(neg1[:], -1.0)
            nc.gpsimd.memset(ident[:], 0.0).then_inc(s_id0, 1)
            pool.wait_ge(s_id0, 1)
            nc.gpsimd.affine_select(out=ident[:], in_=ident[:], compare_op=ALU.not_equal, fill=1.0, base=0,
                                    pattern=[[-1, P]], channel_multiplier=1).then_inc(s_id, 1)
            pool.wait_ge(s_var, 1)
            nc.gpsimd.tensor_tensor(rstd[:], var[:], expo[:], ALU.pow).then_inc(s_rstd, 1)
            for k in range(XP):
                pool.wait_ge(s_g2, k + 1)
                nc.gpsimd.tensor_tensor(G[:, k * Q:(k + 1) * Q, 2 * D:3 * D], rest[:, k % 2],
                                        G[:, k * Q:(k + 1) * Q, D:2 * D], ALU.subtract).then_inc(s_g3, 1)
            pool.wait_ge(s_partH, 1)
            nc.gpsimd.partition_all_reduce(sumH[:], partH[:], P, RADD).then_inc(s_sumH, 1)
            pool.wait_ge(s_sneg, 1)
            nc.gpsimd.partition_all_reduce(snegr[:], sneg[:], P, RMAX).then_inc(s_snegr, 1)
            pool.wait_ge(s_b, 16)
            pool.wait_ge(s_xc, XP)
            for k in range(XP):
                last = nc.gpsimd.tensor_tensor(
                    xs[:, k * Q:(k + 1) * Q, :], xs[:, k * Q:(k + 1) * Q, :],
                    b_row[:].unsqueeze(1).to_broadcast([P, Q, D]), ALU.add)
            last.then_inc(s_xb, 1)

        @block.scalar
        def _(act):
            for k in range(XP + 1):
                if k < XP:
                    act.wait_ge(s_T, k + 1)
                    if k >= 2:
                        act.wait_ge(s_H, k - 1)
                    nc.scalar.activation(hT[:, k % 2].rearrange("p q n -> p (q n)"), ps_T[k % 2], ACT.Relu,
                                         scale=0.5).then_inc(s_hT, 1)
                if k >= 1:
                    act.wait_ge(s_H, k)
                    nc.scalar.copy(HS[:, (k - 1) * Q:k * Q, :].rearrange("p (b u) e -> p b (u e)", b=2),
                                   ps_H[(k - 1) % 2]).then_inc(s_HS, 1)
            act.wait_ge(s_negD, 1)
            nc.scalar.activation(wt[:], d0[:], ACT.Exp, bias=negD[:]).then_inc(s_wt, 1)
            act.wait_ge(s_wr, 1)
            for k in range(XP + 1):
                if k < XP:
                    for t in range(k * Q, (k + 1) * Q):
                        last = nc.scalar.activation(G[:, t, 0:D], HS[:, t, 0:D], ACT.Copy, scale=wr[:, t:t + 1])
                    last.then_inc(s_g1, 1)
                if k >= 1:
                    act.wait_ge(s_rest, k)
                    nc.scalar.copy(G[:, (k - 1) * Q:k * Q, D:2 * D], rest[:, (k - 1) % 2]).then_inc(s_g2, 1)
            with act.Fori(0, GROUPS // 2) as pair:
                for half in range(2):
                    act.wait_ge(s_chunk, pair * (2 * CHUNKS) + (half + 1) * CHUNKS)
                    act.wait_ge(s_comb, pair * 2 + half + 1)
                    for s in range(SUB):
                        nc.scalar.copy(evac[:, s, :], bank[:, half * SUB + s, 0:GC]).then_inc(s_evac, 1)
                    act.wait_ge(s_res, pair * 2 + half + 1)
                    rows = bass.ds((pair * 2 + half) * SUB, SUB)
                    act.dma_start(out_v[:, rows, :], xs[:, rows, :]).then_inc(s_out, 16)
            act.wait_ge(s_out, 16 * GROUPS)
            act.wait_ge(s_flag, 1)
            general = act.value_load(flag[0:1, 0:1], min_val=0, max_val=1)
            with act.If(general != 0):
                with act.Fori(0, T) as s:
                    act.wait_ge(g_score, s + 1)
                    nc.scalar.activation(gen_p, gen_s, ACT.Exp, bias=gen_nmax[:],
                                         accum_out=gen_den[:]).then_inc(g_prob, 1)
                    for k in range(XP):
                        act.wait_ge(g_T, s * XP + k + 1)
                        if k >= 2:
                            act.wait_ge(g_mm, s * XP + k - 1)
                        nc.scalar.copy(hT[:, k % 2].rearrange("p q n -> p (q n)"), ps_T[k % 2]).then_inc(g_pT, 1)
            act.end_ifs()

        @block.vector
        def _(dve):
            chain = [0]

            def link(ins):
                chain[0] += 1
                ins.then_inc(s_dve, 1)
                dve.wait_ge(s_dve, chain[0])

            def means(k):
                dve.wait_ge(s_x[k], 16)
                for t in range(k * Q, (k + 1) * Q):
                    last = nc.vector.bn_stats(stats[:, t, :], xs[:, t, :])
                last.then_inc(s_stats, 1)

            def masks(n, g, c):
                dve.wait_ge(s_adj[c], (g + 1) * 16)
                return nc.vector.tensor_scalar(mask[:, c].rearrange("p q n -> p (q n)"),
                                               adj_int[:, c].rearrange("p q n -> p (q n)"), 0.0, None, ALU.is_gt)

            def rest_of(k):
                dve.wait_ge(s_g1, k + 1)
                if k >= 2:
                    dve.wait_ge(s_g3, k - 1)
                for q in range(Q):
                    t = k * Q + q
                    last = nc.vector.scalar_tensor_tensor(out=rest[:, k % 2, q, :], in0=HS[:, t, 0:D],
                                                          scalar=wr[:, t:t + 1], in1=G[:, t, 0:D],
                                                          op0=ALU.mult, op1=ALU.subtract)
                last.then_inc(s_rest, 1)

            nc.vector.memset(den[:], 0.0).then_inc(s_comb, 1)
            nc.vector.memset(emp[:], 0.0).then_inc(s_evac, 1)
            dve.wait_ge(s_wa, 1)
            nc.vector.tensor_copy(w_ext[:, D:E], ps_wa).then_inc(s_wext, 1)
            means(0)
            for k in range(XP):
                if k + 1 < XP:
                    means(k + 1)
                dve.wait_ge(s_stats, k + 1)
                link(nc.vector.tensor_tensor(sum2[:, k * Q:(k + 1) * Q], stats[:, k * Q:(k + 1) * Q, 1],
                                             stats[:, k * Q:(k + 1) * Q, 4], ALU.add))
                if k >= 2:
                    dve.wait_ge(s_T, k - 1)
                for q in range(Q):
                    t = k * Q + q
                    last = nc.vector.tensor_scalar(xc[:, k % 2, q, :], xs[:, t, :], 2.0, sum2[:, t:t + 1],
                                                   ALU.mult, ALU.subtract)
                last.then_inc(s_xc, 1)
            link(nc.vector.tensor_tensor(dm[:], stats[:, :, 1], stats[:, :, 4], ALU.subtract))
            link(nc.vector.tensor_tensor(var[:], stats[:, :, 2], stats[:, :, 5], ALU.add))
            link(nc.vector.scalar_tensor_tensor(out=dm[:], in0=dm[:], scalar=0.25, in1=dm[:],
                                                op0=ALU.mult, op1=ALU.mult))
            link(nc.vector.tensor_scalar(var[:], var[:], 1.0 / D, EPS, ALU.mult, ALU.add))
            nc.vector.tensor_tensor(var[:], var[:], dm[:], ALU.add).then_inc(s_var, 1)
            masks(0, 0, 0).then_inc(s_mask, 1)
            dve.wait_ge(s_rstd, 1)
            dve.wait_ge(s_HS, XP)
            link(nc.vector.tensor_tensor(d0[:], HS[:, :, D + 1], rstd[:], ALU.mult))
            nc.vector.reduce_max(dmx[:], d0[:], AX_X).then_inc(s_dmx, 1)
            dve.wait_ge(s_dmxT, 1)
            nc.vector.reduce_max(dtop[:], ps_dmx, AX_X).then_inc(s_dtop, 1)
            dve.wait_ge(s_psD, 1)
            nc.vector.tensor_copy(negD[:], ps_negD).then_inc(s_negD, 1)
            masks(1, 0, 1).then_inc(s_mask, 1)
            dve.wait_ge(s_wt, 1)
            nc.vector.tensor_tensor(wr[:], wt[:], rstd[:], ALU.mult).then_inc(s_wr, 1)
            link(nc.vector.tensor_copy(G[:, :, 3 * D], wt[:]))
            link(nc.vector.tensor_tensor(wrest[:], wt[:], G[:, :, 3 * D], ALU.subtract))
            link(nc.vector.tensor_copy(G[:, :, 3 * D + 1], wrest[:]))
            nc.vector.tensor_tensor(G[:, :, 3 * D + 2], wrest[:], G[:, :, 3 * D + 1],
                                    ALU.subtract).then_inc(s_wparts, 1)
            dve.wait_ge(s_wr, 1)
            for k in range(XP):
                rest_of(k)
                if k + 2 < CHUNKS:
                    masks(k + 2, 0, k + 2).then_inc(s_mask, 1)
            link(nc.vector.tensor_scalar(partH[:], HS[:, 0, 0:D], rstd[:, 0:1], None, ALU.mult))
            for t in range(1, T):
                ins = nc.vector.scalar_tensor_tensor(out=partH[:], in0=HS[:, t, 0:D], scalar=rstd[:, t:t + 1],
                                                     in1=partH[:], op0=ALU.mult, op1=ALU.add)
                if t < T - 1:
                    link(ins)
            ins.then_inc(s_partH, 1)
            dve.wait_ge(s_ab, 32)
            dve.wait_ge(s_b, 16)
            for i in range(2):
                last = nc.vector.tensor_tensor(ab[:, i, :], a_row[:, i, :], b_row[:], ALU.mult)
            link(last)
            link(nc.vector.tensor_reduce(ba[:], ab[:], AX_X, ALU.add))
            link(nc.vector.tensor_tensor(s_full[:], HS[:, :, D], rstd[:], ALU.mult))
            link(nc.vector.tensor_scalar(s_full[:], s_full[:], ba[:, 0:1], None, ALU.add))
            nc.vector.tensor_reduce(sneg[:, 0:1], d0[:], AX_X, ALU.min, negate=True)
            nc.vector.tensor_reduce(sneg[:, 1:2], s_full[:], AX_X, ALU.min, negate=True).then_inc(s_sneg, 1)
            dve.wait_ge(s_snegr, 1)
            link(nc.vector.tensor_scalar(low[:, 0:1], snegr[:, 0:1], negD[:], MAX_SPREAD,
                                         ALU.subtract, ALU.is_le))
            link(nc.vector.tensor_tensor(low[:, 1:2], ba[:, 1:2], batt[:], ALU.add))
            link(nc.vector.tensor_scalar(low[:, 1:2], low[:, 1:2], snegr[:, 0:1], snegr[:, 1:2],
                                         ALU.subtract, ALU.subtract))
            link(nc.vector.scalar_tensor_tensor(out=low[:, 0:1], in0=low[:, 1:2], scalar=LOWEST_SCORE,
                                                in1=low[:, 0:1], op0=ALU.is_ge, op1=ALU.mult))
            nc.vector.tensor_scalar(flag[:], low[:, 0:1], 0.0, None, ALU.is_equal).then_inc(s_flag, 1)
            before_loop = chain[0]
            per_group = 5 + SUB

            def combine(g, base):
                def step(i, ins):
                    ins.then_inc(s_dve, 1)
                    dve.wait_ge(s_dve, base + i)
                dve.wait_ge(s_evac, (g + 1) * SUB + 1)
                step(1, nc.vector.tensor_tensor(num[:], evac[:, :, 0:D], evac[:, :, D:2 * D], ALU.add))
                step(2, nc.vector.tensor_tensor(num[:], num[:], evac[:, :, 2 * D:3 * D], ALU.add))
                nc.vector.tensor_reduce(den[:], evac[:, :, 3 * D:3 * D + 3], AX_X, ALU.add).then_inc(s_comb, 1)
                dve.wait_ge(s_comb, g + 2)
                step(3, nc.vector.tensor_scalar(emp[:], den[:], 0.0, None, ALU.is_equal))
                step(4, nc.vector.scalar_tensor_tensor(out=den[:], in0=emp[:], scalar=float(N), in1=den[:],
                                                       op0=ALU.mult, op1=ALU.add))
                step(5, nc.vector.reciprocal(rden[:], den[:]))
                for s in range(SUB):
                    ins = nc.vector.scalar_tensor_tensor(out=num[:, s, :], in0=sumH[:], scalar=emp[:, s:s + 1],
                                                         in1=num[:, s, :], op0=ALU.mult, op1=ALU.add)
                    ins.then_inc(s_dve, 1)
                dve.wait_ge(s_dve, base + 5 + SUB)
                for s in range(SUB):
                    row = xs[:, bass.ds(g * SUB + s, 1), :].rearrange("p o d -> p (o d)")
                    ins = nc.vector.scalar_tensor_tensor(out=row, in0=num[:, s, :], scalar=rden[:, s:s + 1],
                                                         in1=row, op0=ALU.mult, op1=ALU.add)
                ins.then_inc(s_res, 1)

            dve.wait_ge(s_sumH, 1)
            dve.wait_ge(s_xb, 1)
            with dve.Fori(1, GROUPS) as g:
                for c in range(CHUNKS):
                    dve.wait_ge(s_chunk, (g - 1) * CHUNKS + c + 1)
                    masks(None, g, c).then_inc(s_mask, 1)
                    if c == CHUNKS - 2:
                        combine(g - 1, before_loop + (g - 1) * per_group)
            combine(GROUPS - 1, before_loop + (GROUPS - 1) * per_group)
            dve.wait_ge(s_flag, 1)
            general = dve.value_load(flag[0:1, 0:1], min_val=0, max_val=1)
            with dve.If(general != 0):
                dve.wait_ge(s_res, GROUPS)
                nc.vector.tensor_scalar(d_full[:], d0[:], ba[:, 1:2], None, ALU.add).then_inc(g_d, 1)
                for t in range(T):
                    last = nc.vector.scalar_tensor_tensor(out=gen_H[:, t, :], in0=HS[:, t, 0:D],
                                                          scalar=rstd[:, t:t + 1], in1=b_row[:],
                                                          op0=ALU.mult, op1=ALU.add)
                last.then_inc(g_read, 1)
                dve.wait_ge(g_read, 1)
                dve.wait_ge(g_dB, 16)
                with dve.Fori(0, T) as s:
                    dve.wait_ge(g_row, s * 32 + 32)
                    nc.vector.tensor_scalar(gen_s, gen_d, s_full[:, bass.ds(s, 1)], batt[:],
                                            ALU.add, ALU.add).then_inc(g_dve, 1)
                    dve.wait_ge(g_dve, s * 5 + 1)
                    nc.vector.scalar_tensor_tensor(out=gen_p, in0=gen_adj, scalar=0.0, in1=gen_s,
                                                   op0=ALU.is_gt, op1=ALU.mult).then_inc(g_dve, 1)
                    dve.wait_ge(g_dve, s * 5 + 2)
                    nc.vector.tensor_scalar(gen_s, gen_adj, 0.0, 1.0, ALU.is_gt, ALU.subtract).then_inc(g_dve, 1)
                    dve.wait_ge(g_dve, s * 5 + 3)
                    nc.vector.scalar_tensor_tensor(out=gen_s, in0=gen_s, scalar=-NEG_INF, in1=gen_p,
                                                   op0=ALU.mult, op1=ALU.add).then_inc(g_dve, 1)
                    dve.wait_ge(g_dve, s * 5 + 4)
                    nc.vector.tensor_reduce(gen_nmax[:], gen_s, AX_X, ALU.max, negate=True).then_inc(g_score, 1)
                    dve.wait_ge(g_prob, s + 1)
                    nc.vector.reciprocal(gen_rden[:], gen_den[:]).then_inc(g_dve, 1)
                    dve.wait_ge(g_dve, s * 5 + 5)
                    dve.wait_ge(g_mm, s * XP + XP)
                    nc.vector.scalar_tensor_tensor(out=gen_x[:], in0=ps_gen, scalar=gen_rden[:], in1=gen_x[:],
                                                   op0=ALU.mult, op1=ALU.add).then_inc(g_res, 1)
            dve.end_ifs()

        @block.tensor
        def _(pe):
            pe.wait_ge(s_w, 48)
            nc.tensor.matmul(ps_wa, w_t[:], a_sb[:], start=True, stop=True).then_inc(s_wa, 1)
            pe.wait_ge(s_id, 1)
            pe.wait_ge(s_wext, 1)
            for k in range(XP + 1):
                if k < XP:
                    pe.wait_ge(s_xc, k + 1)
                    if k >= 2:
                        pe.wait_ge(s_hT, k - 1)
                    for q in range(Q):
                        last = nc.tensor.transpose(ps_T[k % 2][:, q * P:(q + 1) * P], xc[:, k % 2, q, :], ident[:])
                    last.then_inc(s_T, 1)
                if k >= 1:
                    j = k - 1
                    pe.wait_ge(s_hT, j + 1)
                    if j >= 2:
                        pe.wait_ge(s_HS, j - 1)
                    for q in range(Q):
                        last = nc.tensor.matmul(ps_H[j % 2][:, q // 2, (q % 2) * E:(q % 2 + 1) * E],
                                                hT[:, j % 2, q, :], w_ext[:], start=True, stop=True)
                    last.then_inc(s_H, 1)
            pe.wait_ge(s_dmx, 1)
            nc.tensor.transpose(ps_dmx, dmx[:], ident[:]).then_inc(s_dmxT, 1)
            pe.wait_ge(s_dtop, 1)
            nc.tensor.matmul(ps_negD, neg1[:], dtop[:], start=True, stop=True).then_inc(s_psD, 1)
            pe.wait_ge(s_wparts, 1)
            with pe.Fori(0, GROUPS // 2) as pair:
                for half in range(2):
                    for c in range(CHUNKS):
                        pe.wait_ge(s_g3, c + 1)
                        pe.wait_ge(s_mask, pair * (2 * CHUNKS) + half * CHUNKS + c + 1)
                        if c == 0 and half:
                            pe.wait_ge(s_evac, pair * (2 * SUB) + 1)
                        for q in range(Q):
                            for s in range(SUB):
                                last = nc.tensor.matmul(
                                    bank[:, half * SUB + s, 0:GC], mask[:, c, q, s * P:(s + 1) * P],
                                    G[:, c * Q + q, 0:GC],
                                    start=(c == 0 and q == 0), stop=(c == CHUNKS - 1 and q == Q - 1))
                        last.then_inc(s_chunk, 1)
                pe.wait_ge(s_evac, pair * (2 * SUB) + SUB + 1)
            pe.wait_ge(s_flag, 1)
            general = pe.value_load(flag[0:1, 0:1], min_val=0, max_val=1)
            with pe.If(general != 0):
                with pe.Fori(0, T) as s:
                    pe.wait_ge(g_prob, s + 1)
                    pe.wait_ge(g_read, s + 1)
                    prob = gen_p.rearrange("m (p t) -> m t p", t=T)
                    for k in range(XP + 1):
                        if k < XP:
                            pe.wait_ge(g_pT, s * XP + k - 1) if k >= 2 else None
                            for q in range(Q):
                                last = nc.tensor.transpose(ps_T[k % 2][:, q * P:(q + 1) * P],
                                                           prob[:, k * Q + q, :], ident[:])
                            last.then_inc(g_T, 1)
                        if k >= 1:
                            j = k - 1
                            pe.wait_ge(g_pT, s * XP + j + 1)
                            for q in range(Q):
                                last = nc.tensor.matmul(ps_gen, hT[:, j % 2, q, :], gen_H[:, j * Q + q, :],
                                                        start=(j == 0 and q == 0), stop=(j == XP - 1 and q == Q - 1))
                            last.then_inc(g_mm, 1)
            pe.end_ifs()


def kernel(x, adj, L0_gnn_W_fc, L0_gnn_b_fc, L0_gnn_w_att, L0_gnn_b_att):
    import numpy as np
    import concourse.bacc as bacc
    from concourse.bass_utils import run_bass_kernel_spmd

    x, adj = np.asarray(x), np.asarray(adj)
    w, b = np.asarray(L0_gnn_W_fc), np.asarray(L0_gnn_b_fc)
    a, b_att = np.asarray(L0_gnn_w_att), np.asarray(L0_gnn_b_att)
    n, d = x.shape
    tiles = n // P
    chunks = 8
    adj_t = np.ascontiguousarray(
        adj.reshape(P, tiles // SUB, SUB, P, chunks, tiles // chunks).transpose(1, 4, 3, 5, 2, 0)
    ).reshape(tiles // SUB, chunks, P, tiles // chunks, SUB * P)
    arrays = {
        "x": x, "adj_t": adj_t, "adj": adj, "w_fc": w, "w_fc_t": np.ascontiguousarray(w.T), "b_fc": b,
        "w_att": a, "a_att": np.ascontiguousarray(a.reshape(2, d).T), "b_att": b_att.reshape(1),
    }
    nc = bacc.Bacc("TRN2", target_bir_lowering=False, num_devices=1)
    ins = [nc.dram_tensor(k, v.shape, mybir.dt.from_np(v.dtype), kind="ExternalInput").ap() for k, v in arrays.items()]
    out = nc.dram_tensor("out", x.shape, mybir.dt.from_np(x.dtype), kind="ExternalOutput").ap()
    gnn_kernel(nc, *ins, out)
    return run_bass_kernel_spmd(nc, [arrays], core_ids=[0]).results[0]["out"]
```

```python
from contextlib import ExitStack

import concourse.bass as bass
from concourse import mybir

P = 128
ALU = mybir.AluOpType
ACT = mybir.ActivationFunctionType
BF16 = mybir.dt.bfloat16
F32 = mybir.dt.float32
I32 = mybir.dt.int32
AX_X = mybir.AxisListType.X
RMAX = bass.bass_isa.ReduceOp.max
RADD = bass.bass_isa.ReduceOp.add

SUB = 4
NEG_INF = -1.0e9
EPS = 1.0e-5
TINY = 1.0e-30
MAX_SPREAD = 40.0
LOWEST_SCORE = -9.0e8


def gnn_kernel(nc, x, adj_t, adj, w_fc, w_fc_t, b_fc, w_att, a_att, b_att, out):
    N, D = x.shape
    T = N // P
    GROUPS, CHUNKS = adj_t.shape[0], adj_t.shape[1]
    Q = T // CHUNKS
    XP = T // Q
    QUICK = 2
    UNITS = [(0, 1), (1, 2), (2, 4)] + [(t, t + Q) for t in range(Q, T, Q)]
    E = D + 2
    GP = D + 1
    GC = 3 * GP
    assert D == P and GROUPS * SUB == T and XP == CHUNKS

    with ExitStack() as ctx:
        def sb(name, shape, dt):
            return ctx.enter_context(nc.sbuf_tensor(name, shape, dt))

        def sem(name):
            return ctx.enter_context(nc.semaphore(name))

        adj_int = sb("adj_int", [P, CHUNKS, SUB, Q * P], I32)
        mask = sb("mask", [P, CHUNKS, SUB, Q * P], BF16)
        G_rows = sb("G", [P, T, GC + 1], BF16)
        G = G_rows[:, :, 0:GC].rearrange("p t (k e) -> p t k e", k=3)
        xs = sb("xs", [P, T, D], F32)
        HS = sb("HS", [P, T, E], F32)
        xc = sb("xc", [P, 2, Q, D], F32)
        hT = sb("hT", [P, 2, Q, P], F32)
        rest = sb("rest", [P, 2, Q, D], F32)
        evac_rows = sb("evac", [P, SUB, GC], F32)
        evac = evac_rows[:].rearrange("p s (k e) -> p s k e", k=3)
        num = sb("num", [P, SUB, D], F32)
        w_ext = sb("w_ext", [P, E], F32)
        w_t = sb("w_t", [P, D], F32)
        a_sb = sb("a_sb", [P, 2], F32)
        b_row = sb("b_row", [P, D], F32)
        ident = sb("ident", [P, P], F32)
        neg1 = sb("neg1", [1, P], F32)
        meanH = sb("meanH", [P, D], F32)
        part = sb("part", [P, Q, D], F32)
        acc = sb("acc", [P, 2, D], F32)
        prod = sb("prod", [P, Q, D], F32)
        stats = sb("stats", [P, T, 6], F32)
        mean = sb("mean", [P, T], F32)
        dm = sb("dm", [P, T], F32)
        var = sb("var", [P, T], F32)
        rstd = sb("rstd", [P, T], F32)
        nhalf = sb("nhalf", [P, T], F32)
        rsq = sb("rsq", [P, T], F32)
        seed = sb("seed", [P, T], I32)
        d0 = sb("d0", [P, T], F32)
        wt = sb("wt", [P, T], F32)
        wrest = sb("wrest", [P, T], F32)
        wr = sb("wr", [P, T], F32)
        dmx = sb("dmx", [P, 1], F32)
        dtop = sb("dtop", [1, 1], F32)
        negD = sb("negD", [P, 1], F32)
        den = sb("den", [P, SUB], F32)
        emp = sb("emp", [P, SUB], F32)
        rden = sb("rden", [P, SUB], F32)

        sneg = sb("sneg", [P, 2], F32)
        snegr = sb("snegr", [P, 2], F32)
        a_row = sb("a_row", [P, 2, D], F32)
        ab = sb("ab", [P, 2, D], F32)
        ba = sb("ba", [P, 2], F32)
        batt = sb("batt", [P, 1], F32)
        s_full = sb("s_full", [P, T], F32)
        low = sb("low", [P, 2], F32)
        flag = sb("flag", [P, 1], I32)
        wide = adj_int[:].rearrange("p c s n -> p (c s n)").rearrange("p (b j) -> p b j", b=4)
        gen_adj = wide[:, 0, :]
        gen_d = wide[:, 1, :].bitcast(F32)
        gen_s = wide[:, 2, :].bitcast(F32)
        gen_p = wide[:, 3, :].bitcast(F32)
        gen_H = mask[:].rearrange("p c s n -> p (c s n)").bitcast(F32)[:, 0:T * D].rearrange("p (t d) -> p t d", t=T)
        d_full = sb("d_full", [P, T], F32)
        gen_x = sb("gen_x", [P, D], F32)
        gen_nmax = sb("gen_nmax", [P, 1], F32)
        gen_den = sb("gen_den", [P, 1], F32)
        gen_rden = sb("gen_rden", [P, 1], F32)
        d_line = nc.dram_tensor("d_line", [P, T], F32)

        bank = ctx.enter_context(nc.psum_tensor("bank", [P, 8, 512], F32))
        ps_T = [bank[:, i, :] for i in range(2)]
        ps_H = [bank[:, 2 + 2 * i:4 + 2 * i, 0:2 * E] for i in range(2)]
        ps_gen = bank[:, 2, 0:D]
        ps_wa = bank[:, 6, 0:2]
        ps_dmx = bank[0:1, 6, 128:256]
        ps_negD = bank[:, 7, 0:1]

        s_w = sem("s_w")
        s_b = sem("s_b")
        s_x = [sem(f"s_x{k}") for k in range(XP)]
        s_adj = [sem(f"s_adj{c}") for c in range(CHUNKS)]
        s_last = [sem(f"s_last{s}") for s in range(SUB)]
        s_id0 = sem("s_id0")
        s_id = sem("s_id")
        s_wa = sem("s_wa")
        s_wext = sem("s_wext")
        s_dve = sem("s_dve")
        s_stats = sem("s_stats")
        s_xc = sem("s_xc")
        s_xc_last = sem("s_xc_last")
        s_T = sem("s_T")
        s_hT = sem("s_hT")
        s_H = sem("s_H")
        s_HS = sem("s_HS")
        s_dmx = sem("s_dmx")
        s_dmxT = sem("s_dmxT")
        s_dtop = sem("s_dtop")
        s_psD = sem("s_psD")
        s_negD = sem("s_negD")
        s_wt = sem("s_wt")
        s_wr = sem("s_wr")
        s_wparts = sem("s_wparts")
        s_g1 = sem("s_g1")
        s_rest = sem("s_rest")
        s_g2 = sem("s_g2")
        s_g3 = sem("s_g3")
        s_quick = sem("s_quick")
        s_mask = sem("s_mask")
        s_chunk = sem("s_chunk")
        s_evac = sem("s_evac")
        s_comb = sem("s_comb")
        s_res = sem("s_res")
        s_mean = sem("s_mean")
        s_acc = sem("s_acc")
        s_accs = [sem(f"s_acc{i}") for i in range(2)]
        s_meanH = sem("s_meanH")
        s_pool = sem("s_pool")
        s_xb = sem("s_xb")
        s_out = sem("s_out")

        s_ab = sem("s_ab")
        s_sneg = sem("s_sneg")
        s_snegr = sem("s_snegr")
        s_path = sem("s_path")
        s_flag = sem("s_flag")
        g_d = sem("g_d")
        g_dline = sem("g_dline")
        g_dB = sem("g_dB")
        g_row = sem("g_row")
        g_read = sem("g_read")
        g_dve = sem("g_dve")
        g_score = sem("g_score")
        g_prob = sem("g_prob")
        g_T = sem("g_T")
        g_pT = sem("g_pT")
        g_mm = sem("g_mm")
        g_res = sem("g_res")
        g_out = sem("g_out")

        x_v = x.rearrange("(p t) d -> p t d", p=P)
        out_v = out.rearrange("(p t) d -> p t d", p=P)
        adj_v = adj.rearrange("(p t) j -> p t j", p=P)

        block = ctx.enter_context(nc.Block())

        @block.sync
        def _(sp):
            for k in range(XP):
                sp.dma_start(xs[:, k * Q:(k + 1) * Q, :], x_v[:, k * Q:(k + 1) * Q, :]).then_inc(s_x[k], 16)
                if k == 0:
                    sp.dma_start(w_t[:], w_fc_t).then_inc(s_w, 16)
                    sp.dma_start(a_sb[:], a_att).then_inc(s_w, 16)
                    sp.dma_start(w_ext[:, 0:D], w_fc).then_inc(s_w, 16)
            sp.dma_start(b_row[:], b_fc.partition_broadcast(P)).then_inc(s_b, 16)
            sp.dma_start(a_row[:].rearrange("p c d -> p (c d)"), w_att.partition_broadcast(P)).then_inc(s_ab, 16)
            sp.dma_start(batt[:], b_att.partition_broadcast(P)).then_inc(s_ab, 16)
            for c in range(CHUNKS):
                sp.dma_start(adj_int[:, c], adj_t[0, c]).then_inc(s_adj[c], 16)
            with sp.Fori(1, GROUPS - 1) as g:
                for c in range(CHUNKS):
                    sp.wait_ge(s_mask, (g - 1) * CHUNKS + c + 1)
                    sp.dma_start(adj_int[:, c], adj_t[bass.ds(g, 1), c].rearrange("o p s n -> (o p) s n")).then_inc(s_adj[c], 16)
            for c in range(CHUNKS):
                sp.wait_ge(s_mask, (GROUPS - 2) * CHUNKS + c + 1)
                if c < CHUNKS - 1:
                    sp.dma_start(adj_int[:, c], adj_t[GROUPS - 1, c]).then_inc(s_adj[c], 16)
            for s in range(SUB):
                sp.dma_start(adj_int[:, CHUNKS - 1, s], adj_t[GROUPS - 1, CHUNKS - 1][:, s]).then_inc(s_last[s], 16)
            sp.wait_ge(s_flag, 1)
            general = sp.value_load(flag[0:1, 0:1], min_val=0, max_val=1)
            with sp.If(general != 0):
                sp.wait_ge(g_d, 1)
                sp.dma_start(d_line.ap(), d_full[:]).then_inc(g_dline, 16)
                sp.wait_ge(g_dline, 16)
                sp.dma_start(gen_d, d_line.ap().rearrange("p t -> (p t)").partition_broadcast(P)).then_inc(g_dB, 16)
                sp.wait_ge(s_out, 16 * (GROUPS - 1 + SUB))
                with sp.Fori(0, T) as s:
                    sp.wait_ge(g_read, s + 1)
                    sp.dma_start(gen_adj, adj_v[:, bass.ds(s, 1), :].rearrange("p o j -> p (o j)")).then_inc(g_row, 16)
                    sp.dma_start(gen_x[:], x_v[:, bass.ds(s, 1), :].rearrange("p o d -> p (o d)")).then_inc(g_row, 16)
                    sp.wait_ge(g_res, s + 1)
                    sp.dma_start(out_v[:, bass.ds(s, 1), :].rearrange("p o d -> p (o d)"), gen_x[:]).then_inc(g_out, 16)
                    sp.wait_ge(g_out, s * 16 + 16)
                    sp.sem_inc(g_read, 1)
            sp.end_ifs()

        @block.gpsimd
        def _(pool):
            nc.gpsimd.memset(neg1[:], -1.0)
            nc.gpsimd.memset(ident[:], 0.0).then_inc(s_id0, 1)
            pool.wait_ge(s_id0, 1)
            nc.gpsimd.affine_select(out=ident[:], in_=ident[:], compare_op=ALU.not_equal, fill=1.0, base=0,
                                    pattern=[[-1, P]], channel_multiplier=1).then_inc(s_id, 1)
            for k in range(XP - 1):
                pool.wait_ge(s_mean, k + 1)
                if k >= 2:
                    pool.wait_ge(s_T, k - 1)
                nc.gpsimd.tensor_tensor(xc[:, k % 2], xs[:, k * Q:(k + 1) * Q, :],
                                        mean[:, k * Q:(k + 1) * Q].unsqueeze(2).to_broadcast([P, Q, D]),
                                        ALU.subtract).then_inc(s_xc, 1)
            pool.wait_ge(s_wt, 1)
            nc.gpsimd.tensor_copy(G[:, :, 0, D], wt[:]).then_inc(s_pool, 1)
            pool.wait_ge(s_pool, 1)
            nc.gpsimd.tensor_tensor(wrest[:], wt[:], G[:, :, 0, D], ALU.subtract).then_inc(s_pool, 1)
            pool.wait_ge(s_pool, 2)
            nc.gpsimd.tensor_copy(G[:, :, 1, D], wrest[:]).then_inc(s_pool, 1)
            pool.wait_ge(s_pool, 3)
            nc.gpsimd.tensor_tensor(G[:, :, 2, D], wrest[:], G[:, :, 1, D],
                                    ALU.subtract).then_inc(s_wparts, 1)
            for u, (t0, t1) in list(enumerate(UNITS))[QUICK:]:
                pool.wait_ge(s_g2, u - QUICK + 1)
                nc.gpsimd.tensor_tensor(G[:, t0:t1, 2, 0:D], rest[:, u % 2, 0:t1 - t0],
                                        G[:, t0:t1, 1, 0:D], ALU.subtract).then_inc(s_g3, 1)
            step = 3

            def add(dst, a, b):
                nc.gpsimd.tensor_tensor(dst, a, b, ALU.add).then_inc(s_pool, 1)

            for k in range(XP // 2):
                dst = part if k == 0 else prod
                nc.gpsimd.tensor_tensor(dst[:], HS[:, k * Q:(k + 1) * Q, 0:D],
                                        rstd[:, k * Q:(k + 1) * Q].unsqueeze(2).to_broadcast([P, Q, D]),
                                        ALU.mult).then_inc(s_pool, 1)
                step += 1
                pool.wait_ge(s_pool, step)
                if k > 0:
                    add(part[:], part[:], prod[:])
                    step += 1
                    pool.wait_ge(s_pool, step)
            add(part[:, 0:2], part[:, 0:2], part[:, 2:4])
            pool.wait_ge(s_pool, step + 1)
            pool.wait_ge(s_acc, 2)
            add(part[:, 0:2], part[:, 0:2], acc[:])
            pool.wait_ge(s_pool, step + 2)
            add(part[:, 0], part[:, 0], part[:, 1])
            pool.wait_ge(s_pool, step + 3)
            step += 3
            nc.gpsimd.tensor_scalar(part[:, 0], part[:, 0], 1.0 / N, None, ALU.mult).then_inc(s_pool, 1)
            pool.wait_ge(s_pool, step + 1)
            nc.gpsimd.partition_all_reduce(meanH[:], part[:, 0, :], P, RADD).then_inc(s_meanH, 1)
            pool.wait_ge(s_b, 16)
            pool.wait_ge(s_xc, XP - 1)
            pool.wait_ge(s_xc_last, 1)
            for g in range(GROUPS):
                rows = xs[:, g * SUB:(g + 1) * SUB, :]
                nc.gpsimd.tensor_tensor(rows, rows, b_row[:].unsqueeze(1).to_broadcast([P, SUB, D]),
                                        ALU.add).then_inc(s_xb, 1)
            pool.wait_ge(s_sneg, 1)
            nc.gpsimd.partition_all_reduce(snegr[:], sneg[:], P, RMAX).then_inc(s_snegr, 1)

        @block.scalar
        def _(act):
            for k in range(XP + 1):
                if k < XP:
                    act.wait_ge(s_T, k + 1)
                    if k >= 2:
                        act.wait_ge(s_H, k - 1)
                    nc.scalar.activation(hT[:, k % 2].rearrange("p q n -> p (q n)"), ps_T[k % 2], ACT.Relu).then_inc(s_hT, 1)
                if k >= 1:
                    act.wait_ge(s_H, k)
                    nc.scalar.copy(HS[:, (k - 1) * Q:k * Q, :].rearrange("p (b u) e -> p b (u e)", b=2),
                                   ps_H[(k - 1) % 2]).then_inc(s_HS, 1)
            act.wait_ge(s_negD, 1)
            nc.scalar.activation(wt[:], d0[:], ACT.Exp, bias=negD[:]).then_inc(s_wt, 1)
            act.wait_ge(s_wr, 1)
            for u in range(len(UNITS) + 1):
                if u < len(UNITS):
                    for t in range(*UNITS[u]):
                        last = nc.scalar.activation(G[:, t, 0, 0:D], HS[:, t, 0:D], ACT.Copy, scale=wr[:, t:t + 1])
                    last.then_inc(s_g1, 1)
                if u > QUICK:
                    t0, t1 = UNITS[u - 1]
                    act.wait_ge(s_rest, u)
                    nc.scalar.copy(G[:, t0:t1, 1, 0:D], rest[:, (u - 1) % 2, 0:t1 - t0]).then_inc(s_g2, 1)

            def empty_banks(g, half, products_done):
                act.wait_ge(s_chunk, products_done)
                act.wait_ge(s_comb, g + 1)
                for s in range(SUB):
                    nc.scalar.copy(evac_rows[:, s, :], bank[:, half * SUB + s, 0:GC]).then_inc(s_evac, 1)
                act.wait_ge(s_res, g + 1)
                rows = bass.ds(g * SUB, SUB)
                act.dma_start(out_v[:, rows, :], xs[:, rows, :]).then_inc(s_out, 16)

            with act.Fori(0, GROUPS // 2 - 1) as pair:
                for half in range(2):
                    empty_banks(pair * 2 + half, half, (pair * 2 + half + 1) * CHUNKS)
            empty_banks(GROUPS - 2, 0, (GROUPS - 1) * CHUNKS)
            for s in range(SUB):
                act.wait_ge(s_res, GROUPS - 1 + s + 1)
                row = (GROUPS - 1) * SUB + s
                act.dma_start(out_v[:, row, :], xs[:, row, :]).then_inc(s_out, 16)
            act.wait_ge(s_out, 16 * (GROUPS - 1 + SUB))
            act.wait_ge(s_flag, 1)
            general = act.value_load(flag[0:1, 0:1], min_val=0, max_val=1)
            with act.If(general != 0):
                with act.Fori(0, T) as s:
                    act.wait_ge(g_score, s + 1)
                    nc.scalar.activation(gen_p, gen_s, ACT.Exp, bias=gen_nmax[:],
                                         accum_out=gen_den[:]).then_inc(g_prob, 1)
                    for k in range(XP):
                        act.wait_ge(g_T, s * XP + k + 1)
                        if k >= 2:
                            act.wait_ge(g_mm, s * XP + k - 1)
                        nc.scalar.copy(hT[:, k % 2].rearrange("p q n -> p (q n)"), ps_T[k % 2]).then_inc(g_pT, 1)
            act.end_ifs()

        @block.vector
        def _(dve):
            chain = [0]

            def link(ins):
                chain[0] += 1
                ins.then_inc(s_dve, 1)
                dve.wait_ge(s_dve, chain[0])

            def means(k):
                dve.wait_ge(s_x[k], 16)
                for t in range(k * Q, (k + 1) * Q):
                    last = nc.vector.bn_stats(stats[:, t, :], xs[:, t, :])
                last.then_inc(s_stats, 1)

            def masks(g, c):
                dve.wait_ge(s_adj[c], (g + 1) * 16)
                return nc.vector.tensor_scalar(mask[:, c].rearrange("p s n -> p (s n)"),
                                               adj_int[:, c].rearrange("p s n -> p (s n)"), 0.0, None, ALU.is_gt)

            def rest_of(u):
                dve.wait_ge(s_g1, u + 1)
                if u >= QUICK + 2:
                    dve.wait_ge(s_g3, u - QUICK - 1)
                elif u >= 2:
                    dve.wait_ge(s_quick, u - 1)
                t0, t1 = UNITS[u]
                for t in range(t0, t1):
                    last = nc.vector.scalar_tensor_tensor(out=rest[:, u % 2, t - t0, :], in0=HS[:, t, 0:D],
                                                          scalar=wr[:, t:t + 1], in1=G[:, t, 0, 0:D],
                                                          op0=ALU.mult, op1=ALU.subtract)
                last.then_inc(s_rest, 1)
                if u < QUICK:
                    dve.wait_ge(s_rest, u + 1)
                    link(nc.vector.tensor_copy(G[:, t0:t1, 1, 0:D], rest[:, u % 2, 0:t1 - t0]))
                    nc.vector.tensor_tensor(G[:, t0:t1, 2, 0:D], rest[:, u % 2, 0:t1 - t0],
                                            G[:, t0:t1, 1, 0:D], ALU.subtract).then_inc(s_quick, 1)

            nc.vector.memset(den[:], 0.0).then_inc(s_comb, 1)
            nc.vector.memset(emp[:], 0.0).then_inc(s_evac, 1)
            dve.wait_ge(s_wa, 1)
            nc.vector.tensor_copy(w_ext[:, D:E], ps_wa).then_inc(s_wext, 1)
            means(0)
            for k in range(XP):
                if k + 1 < XP:
                    means(k + 1)
                tiles = slice(k * Q, (k + 1) * Q)
                dve.wait_ge(s_stats, k + 1)
                link(nc.vector.tensor_tensor(dm[:, tiles], stats[:, tiles, 4], stats[:, tiles, 1], ALU.subtract))
                nc.vector.scalar_tensor_tensor(out=mean[:, tiles], in0=dm[:, tiles], scalar=0.5,
                                               in1=stats[:, tiles, 1], op0=ALU.mult, op1=ALU.add).then_inc(s_mean, 1)
            link(nc.vector.tensor_tensor(var[:], stats[:, :, 2], stats[:, :, 5], ALU.add))
            link(nc.vector.scalar_tensor_tensor(out=dm[:], in0=dm[:], scalar=0.25, in1=dm[:],
                                                op0=ALU.mult, op1=ALU.mult))
            link(nc.vector.tensor_scalar(var[:], var[:], 1.0 / D, EPS, ALU.mult, ALU.add))
            link(nc.vector.tensor_tensor(var[:], var[:], dm[:], ALU.add))
            link(nc.vector.tensor_scalar(seed[:], var[:].bitcast(I32), 1, None, ALU.logical_shift_right))
            link(nc.vector.tensor_scalar(rstd[:].bitcast(I32), seed[:], -1.0, float(0x5F3759DF),
                                         ALU.mult, ALU.add))
            link(nc.vector.tensor_scalar(nhalf[:], var[:], -0.5, None, ALU.mult))
            for _ in range(3):
                link(nc.vector.tensor_tensor(rsq[:], rstd[:], rstd[:], ALU.mult))
                link(nc.vector.tensor_tensor(rsq[:], rsq[:], nhalf[:], ALU.mult))
                link(nc.vector.scalar_tensor_tensor(out=rstd[:], in0=rsq[:], scalar=1.5, in1=rstd[:],
                                                    op0=ALU.add, op1=ALU.mult))
            dve.wait_ge(s_mean, XP)
            dve.wait_ge(s_T, XP - 2)
            for q in range(Q):
                t = (XP - 1) * Q + q
                last = nc.vector.tensor_scalar(xc[:, (XP - 1) % 2, q, :], xs[:, t, :], mean[:, t:t + 1], None,
                                               ALU.subtract)
            last.then_inc(s_xc_last, 1)
            masks(0, 0).then_inc(s_mask, 1)
            masks(0, 1).then_inc(s_mask, 1)
            dve.wait_ge(s_HS, XP)
            link(nc.vector.tensor_tensor(d0[:], HS[:, :, D + 1], rstd[:], ALU.mult))
            nc.vector.reduce_max(dmx[:], d0[:], AX_X).then_inc(s_dmx, 1)
            dve.wait_ge(s_dmxT, 1)
            nc.vector.reduce_max(dtop[:], ps_dmx, AX_X).then_inc(s_dtop, 1)
            dve.wait_ge(s_psD, 1)
            nc.vector.tensor_copy(negD[:], ps_negD).then_inc(s_negD, 1)
            dve.wait_ge(s_wt, 1)
            nc.vector.tensor_tensor(wr[:], wt[:], rstd[:], ALU.mult).then_inc(s_wr, 1)
            dve.wait_ge(s_wr, 1)
            for u in range(len(UNITS)):
                rest_of(u)
                c = u - len(UNITS) + CHUNKS
                if c >= 2:
                    masks(0, c).then_inc(s_mask, 1)
            for n, t in enumerate(range(T // 2, T)):
                i, at = n % 2, n // 2
                if at == 0:
                    ins = nc.vector.tensor_scalar(acc[:, i], HS[:, t, 0:D], rstd[:, t:t + 1], None, ALU.mult)
                else:
                    dve.wait_ge(s_accs[i], at)
                    ins = nc.vector.scalar_tensor_tensor(out=acc[:, i], in0=HS[:, t, 0:D], scalar=rstd[:, t:t + 1],
                                                         in1=acc[:, i], op0=ALU.mult, op1=ALU.add)
                ins.then_inc(s_acc if t >= T - 2 else s_accs[i], 1)
            dve.wait_ge(s_ab, 32)
            dve.wait_ge(s_b, 16)
            for i in range(2):
                last = nc.vector.tensor_tensor(ab[:, i, :], a_row[:, i, :], b_row[:], ALU.mult)
            link(last)
            link(nc.vector.tensor_reduce(ba[:], ab[:], AX_X, ALU.add))
            link(nc.vector.tensor_tensor(s_full[:], HS[:, :, D], rstd[:], ALU.mult))
            link(nc.vector.tensor_scalar(s_full[:], s_full[:], ba[:, 0:1], None, ALU.add))
            nc.vector.tensor_reduce(sneg[:, 0:1], d0[:], AX_X, ALU.min, negate=True)
            nc.vector.tensor_reduce(sneg[:, 1:2], s_full[:], AX_X, ALU.min, negate=True).then_inc(s_sneg, 1)
            before_loop = chain[0]
            per_group = 5 + SUB
            AT = 2

            def chained(base):
                def step(i, ins):
                    ins.then_inc(s_dve, 1)
                    dve.wait_ge(s_dve, base + i)
                return step

            def add_parts(g, base):
                step = chained(base)
                dve.wait_ge(s_evac, (g + 1) * SUB + 1)
                step(1, nc.vector.tensor_tensor(num[:], evac[:, :, 0, 0:D], evac[:, :, 1, 0:D], ALU.add))
                step(2, nc.vector.tensor_tensor(num[:], num[:], evac[:, :, 2, 0:D], ALU.add))
                nc.vector.tensor_reduce(den[:], evac[:, :, :, D], AX_X, ALU.add).then_inc(s_comb, 1)
                dve.wait_ge(s_comb, g + 2)

            def combine(g, base):
                step = chained(base)
                nc.vector.tensor_scalar(emp[:], den[:], 0.0, None, ALU.is_equal).then_inc(s_dve, 1)
                step(4, nc.vector.tensor_scalar(rden[:], den[:], TINY, None, ALU.max))
                step(5, nc.vector.reciprocal(rden[:], rden[:]))
                dve.wait_ge(s_xb, g + 1)
                dve.wait_ge(s_meanH, 1)
                for s in range(SUB):
                    row = xs[:, bass.ds(g * SUB + s, 1), :].rearrange("p o d -> p (o d)")
                    ins = nc.vector.scalar_tensor_tensor(out=row, in0=num[:, s, :], scalar=rden[:, s:s + 1],
                                                         in1=row, op0=ALU.mult, op1=ALU.add)
                    ins.then_inc(s_dve, 1)
                dve.wait_ge(s_dve, base + 5 + SUB)
                for s in range(SUB):
                    row = xs[:, bass.ds(g * SUB + s, 1), :].rearrange("p o d -> p (o d)")
                    ins = nc.vector.scalar_tensor_tensor(out=row, in0=meanH[:], scalar=emp[:, s:s + 1],
                                                         in1=row, op0=ALU.mult, op1=ALU.add)
                ins.then_inc(s_res, 1)

            def combine_bank(s, base):
                dve.wait_ge(s_chunk, GROUPS * CHUNKS - 1 + s + 1)
                row = xs[:, (GROUPS - 1) * SUB + s, :]
                col = slice(s, s + 1)
                weight = bank[:, SUB + s, D:D + 1]
                nc.vector.tensor_scalar(den[:, col], weight, TINY, None, ALU.max).then_inc(s_dve, 1)
                nc.vector.tensor_scalar(emp[:, col], weight, 0.0, None, ALU.is_equal).then_inc(s_dve, 1)
                dve.wait_ge(s_dve, base + 1)
                nc.vector.reciprocal(rden[:, col], den[:, col]).then_inc(s_dve, 1)
                dve.wait_ge(s_dve, base + 2)
                nc.vector.scalar_tensor_tensor(out=row, in0=meanH[:], scalar=emp[:, col], in1=row,
                                               op0=ALU.mult, op1=ALU.add).then_inc(s_dve, 1)
                dve.wait_ge(s_dve, base + 4)
                nc.vector.scalar_tensor_tensor(out=row, in0=bank[:, SUB + s, 0:D], scalar=rden[:, col], in1=row,
                                               op0=ALU.mult, op1=ALU.add).then_inc(s_res, 1)

            def choose_path():
                dve.wait_ge(s_snegr, 1)
                nc.vector.tensor_scalar(low[:, 0:1], snegr[:, 0:1], negD[:], MAX_SPREAD,
                                        ALU.subtract, ALU.is_le).then_inc(s_path, 1)
                nc.vector.tensor_tensor(low[:, 1:2], ba[:, 1:2], batt[:], ALU.add).then_inc(s_path, 1)
                dve.wait_ge(s_path, 2)
                nc.vector.tensor_scalar(low[:, 1:2], low[:, 1:2], snegr[:, 0:1], snegr[:, 1:2],
                                        ALU.subtract, ALU.subtract).then_inc(s_path, 1)
                dve.wait_ge(s_path, 3)
                nc.vector.scalar_tensor_tensor(out=low[:, 0:1], in0=low[:, 1:2], scalar=LOWEST_SCORE,
                                               in1=low[:, 0:1], op0=ALU.is_ge, op1=ALU.mult).then_inc(s_path, 1)
                dve.wait_ge(s_path, 4)
                nc.vector.tensor_scalar(flag[:], low[:, 0:1], 0.0, None, ALU.is_equal).then_inc(s_flag, 1)

            with dve.Fori(1, GROUPS - 1) as g:
                for c in range(CHUNKS):
                    dve.wait_ge(s_chunk, (g - 1) * CHUNKS + c + 1)
                    masks(g, c).then_inc(s_mask, 1)
                    if c == AT:
                        add_parts(g - 1, before_loop + (g - 1) * per_group)
                    if c == AT + 1:
                        combine(g - 1, before_loop + (g - 1) * per_group)
            choose_path()
            for c in range(CHUNKS - 1):
                dve.wait_ge(s_chunk, (GROUPS - 2) * CHUNKS + c + 1)
                masks(GROUPS - 1, c).then_inc(s_mask, 1)
                if c == AT:
                    add_parts(GROUPS - 2, before_loop + (GROUPS - 2) * per_group)
                if c == AT + 1:
                    combine(GROUPS - 2, before_loop + (GROUPS - 2) * per_group)
            for s in range(SUB):
                dve.wait_ge(s_last[s], 16)
                nc.vector.tensor_scalar(mask[:, CHUNKS - 1, s], adj_int[:, CHUNKS - 1, s], 0.0, None,
                                        ALU.is_gt).then_inc(s_mask, 1)
            dve.wait_ge(s_xb, GROUPS)
            for s in range(SUB):
                combine_bank(s, before_loop + (GROUPS - 1) * per_group + s * 4)
            dve.wait_ge(s_flag, 1)
            general = dve.value_load(flag[0:1, 0:1], min_val=0, max_val=1)
            with dve.If(general != 0):
                dve.wait_ge(s_res, GROUPS - 1 + SUB)
                nc.vector.tensor_scalar(d_full[:], d0[:], ba[:, 1:2], None, ALU.add).then_inc(g_d, 1)
                for t in range(T):
                    last = nc.vector.scalar_tensor_tensor(out=gen_H[:, t, :], in0=HS[:, t, 0:D],
                                                          scalar=rstd[:, t:t + 1], in1=b_row[:],
                                                          op0=ALU.mult, op1=ALU.add)
                last.then_inc(g_read, 1)
                dve.wait_ge(g_read, 1)
                dve.wait_ge(g_dB, 16)
                with dve.Fori(0, T) as s:
                    dve.wait_ge(g_row, s * 32 + 32)
                    nc.vector.tensor_scalar(gen_s, gen_d, s_full[:, bass.ds(s, 1)], batt[:],
                                            ALU.add, ALU.add).then_inc(g_dve, 1)
                    dve.wait_ge(g_dve, s * 5 + 1)
                    nc.vector.scalar_tensor_tensor(out=gen_p, in0=gen_adj, scalar=0.0, in1=gen_s,
                                                   op0=ALU.is_gt, op1=ALU.mult).then_inc(g_dve, 1)
                    dve.wait_ge(g_dve, s * 5 + 2)
                    nc.vector.tensor_scalar(gen_s, gen_adj, 0.0, 1.0, ALU.is_gt, ALU.subtract).then_inc(g_dve, 1)
                    dve.wait_ge(g_dve, s * 5 + 3)
                    nc.vector.scalar_tensor_tensor(out=gen_s, in0=gen_s, scalar=-NEG_INF, in1=gen_p,
                                                   op0=ALU.mult, op1=ALU.add).then_inc(g_dve, 1)
                    dve.wait_ge(g_dve, s * 5 + 4)
                    nc.vector.tensor_reduce(gen_nmax[:], gen_s, AX_X, ALU.max, negate=True).then_inc(g_score, 1)
                    dve.wait_ge(g_prob, s + 1)
                    nc.vector.reciprocal(gen_rden[:], gen_den[:]).then_inc(g_dve, 1)
                    dve.wait_ge(g_dve, s * 5 + 5)
                    dve.wait_ge(g_mm, s * XP + XP)
                    nc.vector.scalar_tensor_tensor(out=gen_x[:], in0=ps_gen, scalar=gen_rden[:], in1=gen_x[:],
                                                   op0=ALU.mult, op1=ALU.add).then_inc(g_res, 1)
            dve.end_ifs()

        @block.tensor
        def _(pe):
            pe.wait_ge(s_w, 48)
            nc.tensor.matmul(ps_wa, w_t[:], a_sb[:], start=True, stop=True).then_inc(s_wa, 1)
            pe.wait_ge(s_id, 1)
            pe.wait_ge(s_wext, 1)
            for k in range(XP + 1):
                if k < XP:
                    if k < XP - 1:
                        pe.wait_ge(s_xc, k + 1)
                    else:
                        pe.wait_ge(s_xc_last, 1)
                    if k >= 2:
                        pe.wait_ge(s_hT, k - 1)
                    for q in range(Q):
                        last = nc.tensor.transpose(ps_T[k % 2][:, q * P:(q + 1) * P], xc[:, k % 2, q, :], ident[:])
                    last.then_inc(s_T, 1)
                if k >= 1:
                    j = k - 1
                    pe.wait_ge(s_hT, j + 1)
                    if j >= 2:
                        pe.wait_ge(s_HS, j - 1)
                    for q in range(Q):
                        last = nc.tensor.matmul(ps_H[j % 2][:, q // 2, (q % 2) * E:(q % 2 + 1) * E],
                                                hT[:, j % 2, q, :], w_ext[:], start=True, stop=True)
                    last.then_inc(s_H, 1)
            pe.wait_ge(s_dmx, 1)
            nc.tensor.transpose(ps_dmx, dmx[:], ident[:]).then_inc(s_dmxT, 1)
            pe.wait_ge(s_dtop, 1)
            nc.tensor.matmul(ps_negD, neg1[:], dtop[:], start=True, stop=True).then_inc(s_psD, 1)
            pe.wait_ge(s_wparts, 1)

            def products(g, half, c, added=False):
                pe.wait_ge(s_mask, g * CHUNKS + c + 1)
                for q in range(Q):
                    t = c * Q + q
                    starts = [t0 for t0, _ in UNITS]
                    if t in starts:
                        u = starts.index(t)
                        pe.wait_ge(s_quick, u + 1) if u < QUICK else pe.wait_ge(s_g3, u - QUICK + 1)
                    for s in range(SUB):
                        adj01 = mask[:, c, s, q * P:(q + 1) * P]
                        if not added:
                            last = nc.tensor.matmul(bank[:, half * SUB + s, 0:GC], adj01, G_rows[:, t, 0:GC],
                                                    start=(t == 0), stop=(t == T - 1))
                            continue
                        for k in range(3):
                            last = nc.tensor.matmul(bank[:, half * SUB + s, 0:GP], adj01, G[:, t, k, :],
                                                    start=(t == 0 and k == 0), stop=(t == T - 1 and k == 2))
                last.then_inc(s_chunk, 1)

            with pe.Fori(0, GROUPS // 2 - 1) as pair:
                for c in range(CHUNKS):
                    products(pair * 2, 0, c)
                pe.wait_ge(s_evac, pair * (2 * SUB) + 1)
                for c in range(CHUNKS):
                    products(pair * 2 + 1, 1, c)
                pe.wait_ge(s_evac, pair * (2 * SUB) + SUB + 1)
            for c in range(CHUNKS):
                products(GROUPS - 2, 0, c)
            pe.wait_ge(s_evac, (GROUPS - 2) * SUB + 1)
            for c in range(CHUNKS - 1):
                products(GROUPS - 1, 1, c, added=True)
            for s in range(SUB):
                pe.wait_ge(s_mask, GROUPS * CHUNKS - 1 + s + 1)
                for q in range(Q):
                    t = (CHUNKS - 1) * Q + q
                    for k in range(3):
                        last = nc.tensor.matmul(bank[:, SUB + s, 0:GP], mask[:, CHUNKS - 1, s, q * P:(q + 1) * P],
                                                G[:, t, k, :], start=False, stop=(t == T - 1 and k == 2))
                last.then_inc(s_chunk, 1)
            pe.wait_ge(s_flag, 1)
            general = pe.value_load(flag[0:1, 0:1], min_val=0, max_val=1)
            with pe.If(general != 0):
                with pe.Fori(0, T) as s:
                    pe.wait_ge(g_prob, s + 1)
                    pe.wait_ge(g_read, s + 1)
                    prob = gen_p.rearrange("m (p t) -> m t p", t=T)
                    for k in range(XP + 1):
                        if k < XP:
                            pe.wait_ge(g_pT, s * XP + k - 1) if k >= 2 else None
                            for q in range(Q):
                                last = nc.tensor.transpose(ps_T[k % 2][:, q * P:(q + 1) * P],
                                                           prob[:, k * Q + q, :], ident[:])
                            last.then_inc(g_T, 1)
                        if k >= 1:
                            j = k - 1
                            pe.wait_ge(g_pT, s * XP + j + 1)
                            for q in range(Q):
                                last = nc.tensor.matmul(ps_gen, hT[:, j % 2, q, :], gen_H[:, j * Q + q, :],
                                                        start=(j == 0 and q == 0), stop=(j == XP - 1 and q == Q - 1))
                            last.then_inc(g_mm, 1)
            pe.end_ifs()


def kernel(x, adj, L0_gnn_W_fc, L0_gnn_b_fc, L0_gnn_w_att, L0_gnn_b_att):
    import numpy as np
    import concourse.bacc as bacc
    from concourse.bass_utils import run_bass_kernel_spmd

    x, adj = np.asarray(x), np.asarray(adj)
    w, b = np.asarray(L0_gnn_W_fc), np.asarray(L0_gnn_b_fc)
    a, b_att = np.asarray(L0_gnn_w_att), np.asarray(L0_gnn_b_att)
    n, d = x.shape
    tiles = n // P
    chunks = 8
    adj_t = np.ascontiguousarray(
        adj.reshape(P, tiles // SUB, SUB, P, chunks, tiles // chunks).transpose(1, 4, 3, 2, 5, 0)
    ).reshape(tiles // SUB, chunks, P, SUB, tiles // chunks * P)
    arrays = {
        "x": x, "adj_t": adj_t, "adj": adj, "w_fc": w, "w_fc_t": np.ascontiguousarray(w.T), "b_fc": b,
        "w_att": a, "a_att": np.ascontiguousarray(a.reshape(2, d).T), "b_att": b_att.reshape(1),
    }
    nc = bacc.Bacc("TRN2", target_bir_lowering=False, num_devices=1)
    ins = [nc.dram_tensor(k, v.shape, mybir.dt.from_np(v.dtype), kind="ExternalInput").ap() for k, v in arrays.items()]
    out = nc.dram_tensor("out", x.shape, mybir.dt.from_np(x.dtype), kind="ExternalOutput").ap()
    gnn_kernel(nc, *ins, out)
    return run_bass_kernel_spmd(nc, [arrays], core_ids=[0]).results[0]["out"]
```

```python
from contextlib import ExitStack

import concourse.bass as bass
from concourse import mybir

P = 128
ALU = mybir.AluOpType
ACT = mybir.ActivationFunctionType
BF16 = mybir.dt.bfloat16
F32 = mybir.dt.float32
I32 = mybir.dt.int32
AX_X = mybir.AxisListType.X
RMAX = bass.bass_isa.ReduceOp.max
RADD = bass.bass_isa.ReduceOp.add

SUB = 4
NEG_INF = -1.0e9
EPS = 1.0e-5
TINY = 1.0e-30
MAX_SPREAD = 40.0
LOWEST_SCORE = -9.0e8


def gnn_kernel(nc, x, adj_t, adj, w_fc, w_fc_t, b_fc, w_att, a_att, b_att, out):
    N, D = x.shape
    T = N // P
    GROUPS, CHUNKS = adj_t.shape[0], adj_t.shape[1]
    Q = T // CHUNKS
    XP = T // Q
    QUICK = 2
    UNITS = [(0, 1), (1, 2), (2, 4)] + [(t, t + Q) for t in range(Q, T, Q)]
    HE = D + 2
    LAST = GROUPS - 1
    PART = D + 1
    PARTS = 3 * PART
    assert D == P and GROUPS * SUB == T and XP == CHUNKS

    with ExitStack() as ctx:
        def sb(name, shape, dt):
            return ctx.enter_context(nc.sbuf_tensor(name, shape, dt))

        def sem(name):
            return ctx.enter_context(nc.semaphore(name))

        adj_int = sb("adj_int", [P, CHUNKS, SUB, Q * P], I32)
        mask = sb("mask", [P, CHUNKS, SUB, Q * P], BF16)
        wh_rows = sb("wh", [P, T, PARTS + 1], BF16)
        wh = wh_rows[:, :, 0:PARTS].rearrange("p t (k e) -> p t k e", k=3)
        x_sb = sb("x_sb", [P, T, D], F32)
        H_raw = sb("H_raw", [P, T, HE], F32)
        centred = sb("centred", [P, 2, Q, D], F32)
        relu_T = sb("relu_T", [P, 2, Q, P], F32)
        wh_rest = sb("wh_rest", [P, 2, Q, D], F32)
        sums_rows = sb("sums", [P, SUB, PARTS], F32)
        sums = sums_rows[:].rearrange("p s (k e) -> p s k e", k=3)
        total = sb("total", [P, SUB, D], F32)
        w_and_wa = sb("w_and_wa", [P, HE], F32)
        w_T = sb("w_T", [P, D], F32)
        a_cols = sb("a_cols", [P, 2], F32)
        b_row = sb("b_row", [P, D], F32)
        ident = sb("ident", [P, P], F32)
        minus_ones = sb("minus_ones", [1, P], F32)
        mean_H = sb("mean_H", [P, D], F32)
        h_part = sb("h_part", [P, Q, D], F32)
        h_acc = sb("h_acc", [P, 2, D], F32)
        h_prod = sb("h_prod", [P, Q, D], F32)
        stats = sb("stats", [P, T, 6], F32)
        mean = sb("mean", [P, T], F32)
        mean_diff = sb("mean_diff", [P, T], F32)
        var = sb("var", [P, T], F32)
        rstd = sb("rstd", [P, T], F32)
        minus_half_var = sb("minus_half_var", [P, T], F32)
        newton = sb("newton", [P, T], F32)
        seed = sb("seed", [P, T], I32)
        d_raw = sb("d_raw", [P, T], F32)
        w_j = sb("w_j", [P, T], F32)
        w_rest = sb("w_rest", [P, T], F32)
        w_over_std = sb("w_over_std", [P, T], F32)
        d_max = sb("d_max", [P, 1], F32)
        d_top = sb("d_top", [1, 1], F32)
        minus_D = sb("minus_D", [P, 1], F32)
        weight_sum = sb("weight_sum", [P, SUB], F32)
        is_empty = sb("is_empty", [P, SUB], F32)
        inv_sum = sb("inv_sum", [P, SUB], F32)

        neg_mins = sb("neg_mins", [P, 2], F32)
        neg_mins_all = sb("neg_mins_all", [P, 2], F32)
        a_row = sb("a_row", [P, 2, D], F32)
        ab_prod = sb("ab_prod", [P, 2, D], F32)
        b_logits = sb("b_logits", [P, 2], F32)
        b_att_col = sb("b_att_col", [P, 1], F32)
        s_logit = sb("s_logit", [P, T], F32)
        fits = sb("fits", [P, 2], F32)
        flag = sb("flag", [P, 1], I32)
        wide = adj_int[:].rearrange("p c s n -> p (c s n)").rearrange("p (b j) -> p b j", b=4)
        gen_adj = wide[:, 0, :]
        gen_d = wide[:, 1, :].bitcast(F32)
        gen_score = wide[:, 2, :].bitcast(F32)
        gen_prob = wide[:, 3, :].bitcast(F32)
        gen_H = mask[:].rearrange("p c s n -> p (c s n)").bitcast(F32)[:, 0:T * D].rearrange("p (t d) -> p t d", t=T)
        d_logit = sb("d_logit", [P, T], F32)
        gen_x = sb("gen_x", [P, D], F32)
        gen_neg_max = sb("gen_neg_max", [P, 1], F32)
        gen_sum = sb("gen_sum", [P, 1], F32)
        gen_inv_sum = sb("gen_inv_sum", [P, 1], F32)
        d_scratch = nc.dram_tensor("d_scratch", [P, T], F32)

        bank = ctx.enter_context(nc.psum_tensor("bank", [P, 8, 512], F32))
        ps_transposed = [bank[:, i, :] for i in range(2)]
        ps_H = [bank[:, 2 + 2 * i:4 + 2 * i, 0:2 * HE] for i in range(2)]
        ps_gen = bank[:, 2, 0:D]
        ps_wa = bank[:, 6, 0:2]
        ps_d_max = bank[0:1, 6, 128:256]
        ps_minus_D = bank[:, 7, 0:1]

        w_landed = sem("w_landed")
        b_landed = sem("b_landed")
        x_landed = [sem(f"x_landed{k}") for k in range(XP)]
        adj_landed = [sem(f"adj_landed{c}") for c in range(CHUNKS)]
        adj_part_landed = {(c, s): sem(f"adj_part_landed{c}_{s}") for c in range(CHUNKS) for s in range(SUB)}
        ident_cleared = sem("ident_cleared")
        ident_ready = sem("ident_ready")
        wa_in_psum = sem("wa_in_psum")
        wa_ready = sem("wa_ready")
        vector_chain = sem("vector_chain")
        stats_ready = sem("stats_ready")
        centred_ready = sem("centred_ready")
        last_centred_ready = sem("last_centred_ready")
        transposed = sem("transposed")
        relu_ready = sem("relu_ready")
        H_in_psum = sem("H_in_psum")
        H_ready = sem("H_ready")
        d_max_ready = sem("d_max_ready")
        d_max_row_ready = sem("d_max_row_ready")
        d_top_ready = sem("d_top_ready")
        D_in_psum = sem("D_in_psum")
        D_ready = sem("D_ready")
        w_ready = sem("w_ready")
        w_over_std_ready = sem("w_over_std_ready")
        w_parts_ready = sem("w_parts_ready")
        first_parts = sem("first_parts")
        rest_ready = sem("rest_ready")
        second_parts = sem("second_parts")
        third_parts = sem("third_parts")
        quick_units = sem("quick_units")
        masks_ready = sem("masks_ready")
        chunks_done = sem("chunks_done")
        banks_emptied = sem("banks_emptied")
        sums_read = sem("sums_read")
        results_ready = sem("results_ready")
        means_ready = sem("means_ready")
        h_acc_ready = sem("h_acc_ready")
        h_acc_steps = [sem(f"h_acc_ready{i}") for i in range(2)]
        mean_H_ready = sem("mean_H_ready")
        pool_chain = sem("pool_chain")
        x_plus_b_ready = sem("x_plus_b_ready")
        out_stored = sem("out_stored")

        att_landed = sem("att_landed")
        neg_mins_ready = sem("neg_mins_ready")
        neg_mins_all_ready = sem("neg_mins_all_ready")
        path_chain = sem("path_chain")
        path_chosen = sem("path_chosen")
        gen_d_ready = sem("gen_d_ready")
        gen_d_stored = sem("gen_d_stored")
        gen_d_landed = sem("gen_d_landed")
        gen_rows_landed = sem("gen_rows_landed")
        gen_tile_free = sem("gen_tile_free")
        gen_vector_chain = sem("gen_vector_chain")
        gen_scores_ready = sem("gen_scores_ready")
        gen_probs_ready = sem("gen_probs_ready")
        gen_transposed = sem("gen_transposed")
        gen_probs_T_ready = sem("gen_probs_T_ready")
        gen_products = sem("gen_products")
        gen_result_ready = sem("gen_result_ready")
        gen_out_stored = sem("gen_out_stored")

        x_v = x.rearrange("(p t) d -> p t d", p=P)
        out_v = out.rearrange("(p t) d -> p t d", p=P)
        adj_v = adj.rearrange("(p t) j -> p t j", p=P)

        block = ctx.enter_context(nc.Block())

        @block.sync
        def _(sp):
            for k in range(XP):
                sp.dma_start(x_sb[:, k * Q:(k + 1) * Q, :], x_v[:, k * Q:(k + 1) * Q, :]).then_inc(x_landed[k], 16)
                if k == 0:
                    sp.dma_start(w_T[:], w_fc_t).then_inc(w_landed, 16)
                    sp.dma_start(a_cols[:], a_att).then_inc(w_landed, 16)
                    sp.dma_start(w_and_wa[:, 0:D], w_fc).then_inc(w_landed, 16)
            sp.dma_start(b_row[:], b_fc.partition_broadcast(P)).then_inc(b_landed, 16)
            sp.dma_start(a_row[:].rearrange("p c d -> p (c d)"), w_att.partition_broadcast(P)).then_inc(att_landed, 16)
            sp.dma_start(b_att_col[:], b_att.partition_broadcast(P)).then_inc(att_landed, 16)
            for c in range(CHUNKS):
                sp.dma_start(adj_int[:, c], adj_t[0, c]).then_inc(adj_landed[c], 16)
            with sp.Fori(1, GROUPS - 1) as g:
                for c in range(CHUNKS):
                    sp.wait_ge(masks_ready, (g - 1) * CHUNKS + c + 1)
                    sp.dma_start(adj_int[:, c], adj_t[bass.ds(g, 1), c].rearrange("o p s n -> (o p) s n")
                                 ).then_inc(adj_landed[c], 16)
            for c in range(CHUNKS):
                sp.wait_ge(masks_ready, (LAST - 1) * CHUNKS + c + 1)
                for s in range(SUB):
                    sp.dma_start(adj_int[:, c, s], adj_t[LAST, c][:, s]).then_inc(adj_part_landed[c, s], 16)
            sp.wait_ge(path_chosen, 1)
            general = sp.value_load(flag[0:1, 0:1], min_val=0, max_val=1)
            with sp.If(general != 0):
                sp.wait_ge(gen_d_ready, 1)
                sp.dma_start(d_scratch.ap(), d_logit[:]).then_inc(gen_d_stored, 16)
                sp.wait_ge(gen_d_stored, 16)
                sp.dma_start(gen_d, d_scratch.ap().rearrange("p t -> (p t)").partition_broadcast(P)).then_inc(gen_d_landed, 16)
                sp.wait_ge(out_stored, 16 * (GROUPS - 1 + SUB))
                with sp.Fori(0, T) as s:
                    sp.wait_ge(gen_tile_free, s + 1)
                    sp.dma_start(gen_adj, adj_v[:, bass.ds(s, 1), :].rearrange("p o j -> p (o j)")).then_inc(gen_rows_landed, 16)
                    sp.dma_start(gen_x[:], x_v[:, bass.ds(s, 1), :].rearrange("p o d -> p (o d)")).then_inc(gen_rows_landed, 16)
                    sp.wait_ge(gen_result_ready, s + 1)
                    sp.dma_start(out_v[:, bass.ds(s, 1), :].rearrange("p o d -> p (o d)"), gen_x[:]).then_inc(gen_out_stored, 16)
                    sp.wait_ge(gen_out_stored, s * 16 + 16)
                    sp.sem_inc(gen_tile_free, 1)
            sp.end_ifs()

        @block.gpsimd
        def _(pool):
            nc.gpsimd.memset(minus_ones[:], -1.0)
            nc.gpsimd.memset(ident[:], 0.0).then_inc(ident_cleared, 1)
            pool.wait_ge(ident_cleared, 1)
            nc.gpsimd.affine_select(out=ident[:], in_=ident[:], compare_op=ALU.not_equal, fill=1.0, base=0,
                                    pattern=[[-1, P]], channel_multiplier=1).then_inc(ident_ready, 1)
            for k in range(XP - 1):
                pool.wait_ge(means_ready, k + 1)
                if k >= 2:
                    pool.wait_ge(transposed, k - 1)
                nc.gpsimd.tensor_tensor(centred[:, k % 2], x_sb[:, k * Q:(k + 1) * Q, :],
                                        mean[:, k * Q:(k + 1) * Q].unsqueeze(2).to_broadcast([P, Q, D]),
                                        ALU.subtract).then_inc(centred_ready, 1)
            pool.wait_ge(w_ready, 1)
            nc.gpsimd.tensor_copy(wh[:, :, 0, D], w_j[:]).then_inc(pool_chain, 1)
            pool.wait_ge(pool_chain, 1)
            nc.gpsimd.tensor_tensor(w_rest[:], w_j[:], wh[:, :, 0, D], ALU.subtract).then_inc(pool_chain, 1)
            pool.wait_ge(pool_chain, 2)
            nc.gpsimd.tensor_copy(wh[:, :, 1, D], w_rest[:]).then_inc(pool_chain, 1)
            pool.wait_ge(pool_chain, 3)
            nc.gpsimd.tensor_tensor(wh[:, :, 2, D], w_rest[:], wh[:, :, 1, D],
                                    ALU.subtract).then_inc(w_parts_ready, 1)
            for u, (t0, t1) in list(enumerate(UNITS))[QUICK:]:
                pool.wait_ge(second_parts, u - QUICK + 1)
                nc.gpsimd.tensor_tensor(wh[:, t0:t1, 2, 0:D], wh_rest[:, u % 2, 0:t1 - t0],
                                        wh[:, t0:t1, 1, 0:D], ALU.subtract).then_inc(third_parts, 1)
            step = 3

            def add(dst, a, b):
                nc.gpsimd.tensor_tensor(dst, a, b, ALU.add).then_inc(pool_chain, 1)

            for k in range(XP // 2):
                dst = h_part if k == 0 else h_prod
                nc.gpsimd.tensor_tensor(dst[:], H_raw[:, k * Q:(k + 1) * Q, 0:D],
                                        rstd[:, k * Q:(k + 1) * Q].unsqueeze(2).to_broadcast([P, Q, D]),
                                        ALU.mult).then_inc(pool_chain, 1)
                step += 1
                pool.wait_ge(pool_chain, step)
                if k > 0:
                    add(h_part[:], h_part[:], h_prod[:])
                    step += 1
                    pool.wait_ge(pool_chain, step)
            add(h_part[:, 0:2], h_part[:, 0:2], h_part[:, 2:4])
            pool.wait_ge(pool_chain, step + 1)
            pool.wait_ge(h_acc_ready, 2)
            add(h_part[:, 0:2], h_part[:, 0:2], h_acc[:])
            pool.wait_ge(pool_chain, step + 2)
            add(h_part[:, 0], h_part[:, 0], h_part[:, 1])
            pool.wait_ge(pool_chain, step + 3)
            step += 3
            nc.gpsimd.tensor_scalar(h_part[:, 0], h_part[:, 0], 1.0 / N, None, ALU.mult).then_inc(pool_chain, 1)
            pool.wait_ge(pool_chain, step + 1)
            nc.gpsimd.partition_all_reduce(mean_H[:], h_part[:, 0, :], P, RADD).then_inc(mean_H_ready, 1)
            pool.wait_ge(b_landed, 16)
            pool.wait_ge(centred_ready, XP - 1)
            pool.wait_ge(last_centred_ready, 1)
            for g in range(GROUPS):
                rows = x_sb[:, g * SUB:(g + 1) * SUB, :]
                nc.gpsimd.tensor_tensor(rows, rows, b_row[:].unsqueeze(1).to_broadcast([P, SUB, D]),
                                        ALU.add).then_inc(x_plus_b_ready, 1)
            pool.wait_ge(neg_mins_ready, 1)
            nc.gpsimd.partition_all_reduce(neg_mins_all[:], neg_mins[:], P, RMAX).then_inc(neg_mins_all_ready, 1)

        @block.scalar
        def _(act):
            for k in range(XP + 1):
                if k < XP:
                    act.wait_ge(transposed, k + 1)
                    if k >= 2:
                        act.wait_ge(H_in_psum, k - 1)
                    nc.scalar.activation(relu_T[:, k % 2].rearrange("p q n -> p (q n)"), ps_transposed[k % 2], ACT.Relu).then_inc(relu_ready, 1)
                if k >= 1:
                    act.wait_ge(H_in_psum, k)
                    nc.scalar.copy(H_raw[:, (k - 1) * Q:k * Q, :].rearrange("p (b u) e -> p b (u e)", b=2),
                                   ps_H[(k - 1) % 2]).then_inc(H_ready, 1)
            act.wait_ge(D_ready, 1)
            nc.scalar.activation(w_j[:], d_raw[:], ACT.Exp, bias=minus_D[:]).then_inc(w_ready, 1)
            act.wait_ge(w_over_std_ready, 1)
            for u in range(len(UNITS) + 1):
                if u < len(UNITS):
                    for t in range(*UNITS[u]):
                        last = nc.scalar.activation(wh[:, t, 0, 0:D], H_raw[:, t, 0:D], ACT.Copy, scale=w_over_std[:, t:t + 1])
                    last.then_inc(first_parts, 1)
                if u > QUICK:
                    t0, t1 = UNITS[u - 1]
                    act.wait_ge(rest_ready, u)
                    nc.scalar.copy(wh[:, t0:t1, 1, 0:D], wh_rest[:, (u - 1) % 2, 0:t1 - t0]).then_inc(second_parts, 1)

            def empty_banks(g, half, products_done):
                act.wait_ge(chunks_done, products_done)
                act.wait_ge(sums_read, g + 1)
                for s in range(SUB):
                    nc.scalar.copy(sums_rows[:, s, :], bank[:, half * SUB + s, 0:PARTS]).then_inc(banks_emptied, 1)
                act.wait_ge(results_ready, g + 1)
                rows = bass.ds(g * SUB, SUB)
                act.dma_start(out_v[:, rows, :], x_sb[:, rows, :]).then_inc(out_stored, 16)

            with act.Fori(0, GROUPS // 2 - 1) as pair:
                for half in range(2):
                    empty_banks(pair * 2 + half, half, (pair * 2 + half + 1) * CHUNKS)
            empty_banks(GROUPS - 2, 0, (GROUPS - 1) * CHUNKS)
            for s in range(SUB):
                act.wait_ge(results_ready, GROUPS - 1 + s + 1)
                row = (GROUPS - 1) * SUB + s
                act.dma_start(out_v[:, row, :], x_sb[:, row, :]).then_inc(out_stored, 16)
            act.wait_ge(out_stored, 16 * (GROUPS - 1 + SUB))
            act.wait_ge(path_chosen, 1)
            general = act.value_load(flag[0:1, 0:1], min_val=0, max_val=1)
            with act.If(general != 0):
                with act.Fori(0, T) as s:
                    act.wait_ge(gen_scores_ready, s + 1)
                    nc.scalar.activation(gen_prob, gen_score, ACT.Exp, bias=gen_neg_max[:],
                                         accum_out=gen_sum[:]).then_inc(gen_probs_ready, 1)
                    for k in range(XP):
                        act.wait_ge(gen_transposed, s * XP + k + 1)
                        if k >= 2:
                            act.wait_ge(gen_products, s * XP + k - 1)
                        nc.scalar.copy(relu_T[:, k % 2].rearrange("p q n -> p (q n)"), ps_transposed[k % 2]).then_inc(gen_probs_T_ready, 1)
            act.end_ifs()

        @block.vector
        def _(dve):
            chain = [0]

            def link(ins):
                chain[0] += 1
                ins.then_inc(vector_chain, 1)
                dve.wait_ge(vector_chain, chain[0])

            def row_stats(k):
                dve.wait_ge(x_landed[k], 16)
                for t in range(k * Q, (k + 1) * Q):
                    last = nc.vector.bn_stats(stats[:, t, :], x_sb[:, t, :])
                last.then_inc(stats_ready, 1)

            def masks(g, c):
                dve.wait_ge(adj_landed[c], (g + 1) * 16)
                return nc.vector.tensor_scalar(mask[:, c].rearrange("p s n -> p (s n)"),
                                               adj_int[:, c].rearrange("p s n -> p (s n)"), 0.0, None, ALU.is_gt)

            def rest_of(u):
                dve.wait_ge(first_parts, u + 1)
                if u >= QUICK + 2:
                    dve.wait_ge(third_parts, u - QUICK - 1)
                elif u >= 2:
                    dve.wait_ge(quick_units, u - 1)
                t0, t1 = UNITS[u]
                for t in range(t0, t1):
                    last = nc.vector.scalar_tensor_tensor(out=wh_rest[:, u % 2, t - t0, :], in0=H_raw[:, t, 0:D],
                                                          scalar=w_over_std[:, t:t + 1], in1=wh[:, t, 0, 0:D],
                                                          op0=ALU.mult, op1=ALU.subtract)
                last.then_inc(rest_ready, 1)
                if u < QUICK:
                    dve.wait_ge(rest_ready, u + 1)
                    link(nc.vector.tensor_copy(wh[:, t0:t1, 1, 0:D], wh_rest[:, u % 2, 0:t1 - t0]))
                    nc.vector.tensor_tensor(wh[:, t0:t1, 2, 0:D], wh_rest[:, u % 2, 0:t1 - t0],
                                            wh[:, t0:t1, 1, 0:D], ALU.subtract).then_inc(quick_units, 1)

            nc.vector.memset(weight_sum[:], 0.0).then_inc(sums_read, 1)
            nc.vector.memset(is_empty[:], 0.0).then_inc(banks_emptied, 1)
            dve.wait_ge(wa_in_psum, 1)
            nc.vector.tensor_copy(w_and_wa[:, D:HE], ps_wa).then_inc(wa_ready, 1)
            row_stats(0)
            for k in range(XP):
                if k + 1 < XP:
                    row_stats(k + 1)
                tiles = slice(k * Q, (k + 1) * Q)
                dve.wait_ge(stats_ready, k + 1)
                link(nc.vector.tensor_tensor(mean_diff[:, tiles], stats[:, tiles, 4], stats[:, tiles, 1], ALU.subtract))
                nc.vector.scalar_tensor_tensor(out=mean[:, tiles], in0=mean_diff[:, tiles], scalar=0.5,
                                               in1=stats[:, tiles, 1], op0=ALU.mult, op1=ALU.add).then_inc(means_ready, 1)
            link(nc.vector.tensor_tensor(var[:], stats[:, :, 2], stats[:, :, 5], ALU.add))
            link(nc.vector.scalar_tensor_tensor(out=mean_diff[:], in0=mean_diff[:], scalar=0.25, in1=mean_diff[:],
                                                op0=ALU.mult, op1=ALU.mult))
            link(nc.vector.tensor_scalar(var[:], var[:], 1.0 / D, EPS, ALU.mult, ALU.add))
            link(nc.vector.tensor_tensor(var[:], var[:], mean_diff[:], ALU.add))
            link(nc.vector.tensor_scalar(seed[:], var[:].bitcast(I32), 1, None, ALU.logical_shift_right))
            link(nc.vector.tensor_scalar(rstd[:].bitcast(I32), seed[:], -1.0, float(0x5F3759DF),
                                         ALU.mult, ALU.add))
            link(nc.vector.tensor_scalar(minus_half_var[:], var[:], -0.5, None, ALU.mult))
            for _ in range(3):
                link(nc.vector.tensor_tensor(newton[:], rstd[:], rstd[:], ALU.mult))
                link(nc.vector.tensor_tensor(newton[:], newton[:], minus_half_var[:], ALU.mult))
                link(nc.vector.scalar_tensor_tensor(out=rstd[:], in0=newton[:], scalar=1.5, in1=rstd[:],
                                                    op0=ALU.add, op1=ALU.mult))
            dve.wait_ge(means_ready, XP)
            dve.wait_ge(transposed, XP - 2)
            for q in range(Q):
                t = (XP - 1) * Q + q
                last = nc.vector.tensor_scalar(centred[:, (XP - 1) % 2, q, :], x_sb[:, t, :], mean[:, t:t + 1], None,
                                               ALU.subtract)
            last.then_inc(last_centred_ready, 1)
            masks(0, 0).then_inc(masks_ready, 1)
            masks(0, 1).then_inc(masks_ready, 1)
            dve.wait_ge(H_ready, XP)
            link(nc.vector.tensor_tensor(d_raw[:], H_raw[:, :, D + 1], rstd[:], ALU.mult))
            nc.vector.reduce_max(d_max[:], d_raw[:], AX_X).then_inc(d_max_ready, 1)
            dve.wait_ge(d_max_row_ready, 1)
            nc.vector.reduce_max(d_top[:], ps_d_max, AX_X).then_inc(d_top_ready, 1)
            dve.wait_ge(D_in_psum, 1)
            nc.vector.tensor_copy(minus_D[:], ps_minus_D).then_inc(D_ready, 1)
            dve.wait_ge(w_ready, 1)
            nc.vector.tensor_tensor(w_over_std[:], w_j[:], rstd[:], ALU.mult).then_inc(w_over_std_ready, 1)
            dve.wait_ge(w_over_std_ready, 1)
            for u in range(len(UNITS)):
                rest_of(u)
                c = u - len(UNITS) + CHUNKS
                if c >= 2:
                    masks(0, c).then_inc(masks_ready, 1)
            for n, t in enumerate(range(T // 2, T)):
                i, at = n % 2, n // 2
                if at == 0:
                    ins = nc.vector.tensor_scalar(h_acc[:, i], H_raw[:, t, 0:D], rstd[:, t:t + 1], None, ALU.mult)
                else:
                    dve.wait_ge(h_acc_steps[i], at)
                    ins = nc.vector.scalar_tensor_tensor(out=h_acc[:, i], in0=H_raw[:, t, 0:D], scalar=rstd[:, t:t + 1],
                                                         in1=h_acc[:, i], op0=ALU.mult, op1=ALU.add)
                ins.then_inc(h_acc_ready if t >= T - 2 else h_acc_steps[i], 1)
            dve.wait_ge(att_landed, 32)
            dve.wait_ge(b_landed, 16)
            for i in range(2):
                last = nc.vector.tensor_tensor(ab_prod[:, i, :], a_row[:, i, :], b_row[:], ALU.mult)
            link(last)
            link(nc.vector.tensor_reduce(b_logits[:], ab_prod[:], AX_X, ALU.add))
            link(nc.vector.tensor_tensor(s_logit[:], H_raw[:, :, D], rstd[:], ALU.mult))
            link(nc.vector.tensor_scalar(s_logit[:], s_logit[:], b_logits[:, 0:1], None, ALU.add))
            nc.vector.tensor_reduce(neg_mins[:, 0:1], d_raw[:], AX_X, ALU.min, negate=True)
            nc.vector.tensor_reduce(neg_mins[:, 1:2], s_logit[:], AX_X, ALU.min, negate=True).then_inc(neg_mins_ready, 1)
            before_loop = chain[0]
            per_group = 5 + SUB
            COMBINE_AT = 2

            def chained(base):
                def step(i, ins):
                    ins.then_inc(vector_chain, 1)
                    dve.wait_ge(vector_chain, base + i)
                return step

            def add_parts(g, base):
                step = chained(base)
                dve.wait_ge(banks_emptied, (g + 1) * SUB + 1)
                step(1, nc.vector.tensor_tensor(total[:], sums[:, :, 0, 0:D], sums[:, :, 1, 0:D], ALU.add))
                step(2, nc.vector.tensor_tensor(total[:], total[:], sums[:, :, 2, 0:D], ALU.add))
                nc.vector.tensor_reduce(weight_sum[:], sums[:, :, :, D], AX_X, ALU.add).then_inc(sums_read, 1)
                dve.wait_ge(sums_read, g + 2)

            def combine(g, base):
                step = chained(base)
                nc.vector.tensor_scalar(is_empty[:], weight_sum[:], 0.0, None, ALU.is_equal).then_inc(vector_chain, 1)
                step(4, nc.vector.tensor_scalar(inv_sum[:], weight_sum[:], TINY, None, ALU.max))
                step(5, nc.vector.reciprocal(inv_sum[:], inv_sum[:]))
                dve.wait_ge(x_plus_b_ready, g + 1)
                for s in range(SUB):
                    row = x_sb[:, bass.ds(g * SUB + s, 1), :].rearrange("p o d -> p (o d)")
                    ins = nc.vector.scalar_tensor_tensor(out=row, in0=total[:, s, :], scalar=inv_sum[:, s:s + 1],
                                                         in1=row, op0=ALU.mult, op1=ALU.add)
                    ins.then_inc(vector_chain, 1)

            def mean_for_empty(g, base):
                dve.wait_ge(vector_chain, base + 5 + SUB)
                dve.wait_ge(mean_H_ready, 1)
                for s in range(SUB):
                    row = x_sb[:, bass.ds(g * SUB + s, 1), :].rearrange("p o d -> p (o d)")
                    ins = nc.vector.scalar_tensor_tensor(out=row, in0=mean_H[:], scalar=is_empty[:, s:s + 1],
                                                         in1=row, op0=ALU.mult, op1=ALU.add)
                ins.then_inc(results_ready, 1)

            def combine_bank(s, base):
                dve.wait_ge(chunks_done, LAST * CHUNKS + s + 1)
                dve.wait_ge(x_plus_b_ready, GROUPS)
                row = x_sb[:, (GROUPS - 1) * SUB + s, :]
                col = slice(s, s + 1)
                weight = bank[:, SUB + s, D:D + 1]
                nc.vector.tensor_scalar(weight_sum[:, col], weight, TINY, None, ALU.max).then_inc(vector_chain, 1)
                nc.vector.tensor_scalar(is_empty[:, col], weight, 0.0, None, ALU.is_equal).then_inc(vector_chain, 1)
                dve.wait_ge(vector_chain, base + 1)
                nc.vector.reciprocal(inv_sum[:, col], weight_sum[:, col]).then_inc(vector_chain, 1)
                dve.wait_ge(vector_chain, base + 2)
                nc.vector.scalar_tensor_tensor(out=row, in0=mean_H[:], scalar=is_empty[:, col], in1=row,
                                               op0=ALU.mult, op1=ALU.add).then_inc(vector_chain, 1)
                dve.wait_ge(vector_chain, base + 4)
                nc.vector.scalar_tensor_tensor(out=row, in0=bank[:, SUB + s, 0:D], scalar=inv_sum[:, col], in1=row,
                                               op0=ALU.mult, op1=ALU.add).then_inc(results_ready, 1)

            def choose_path():
                dve.wait_ge(neg_mins_all_ready, 1)
                nc.vector.tensor_scalar(fits[:, 0:1], neg_mins_all[:, 0:1], minus_D[:], MAX_SPREAD,
                                        ALU.subtract, ALU.is_le).then_inc(path_chain, 1)
                nc.vector.tensor_tensor(fits[:, 1:2], b_logits[:, 1:2], b_att_col[:], ALU.add).then_inc(path_chain, 1)
                dve.wait_ge(path_chain, 2)
                nc.vector.tensor_scalar(fits[:, 1:2], fits[:, 1:2], neg_mins_all[:, 0:1], neg_mins_all[:, 1:2],
                                        ALU.subtract, ALU.subtract).then_inc(path_chain, 1)
                dve.wait_ge(path_chain, 3)
                nc.vector.scalar_tensor_tensor(out=fits[:, 0:1], in0=fits[:, 1:2], scalar=LOWEST_SCORE,
                                               in1=fits[:, 0:1], op0=ALU.is_ge, op1=ALU.mult).then_inc(path_chain, 1)
                dve.wait_ge(path_chain, 4)
                nc.vector.tensor_scalar(flag[:], fits[:, 0:1], 0.0, None, ALU.is_equal).then_inc(path_chosen, 1)

            with dve.Fori(1, GROUPS - 1) as g:
                for c in range(CHUNKS):
                    dve.wait_ge(chunks_done, (g - 1) * CHUNKS + c + 1)
                    masks(g, c).then_inc(masks_ready, 1)
                    if c == COMBINE_AT:
                        add_parts(g - 1, before_loop + (g - 1) * per_group)
                    if c == COMBINE_AT + 1:
                        combine(g - 1, before_loop + (g - 1) * per_group)
                    if c == COMBINE_AT + 2:
                        mean_for_empty(g - 1, before_loop + (g - 1) * per_group)
            choose_path()
            before = before_loop + (LAST - 1) * per_group
            for c in range(CHUNKS):
                dve.wait_ge(chunks_done, (LAST - 1) * CHUNKS + c + 1)
                for s in range(SUB):
                    dve.wait_ge(adj_part_landed[c, s], 16)
                    nc.vector.tensor_scalar(mask[:, c, s], adj_int[:, c, s], 0.0, None,
                                            ALU.is_gt).then_inc(masks_ready, 1)
                    if c == CHUNKS - 1 and s >= 2:
                        combine_bank(s - 2, before + per_group + (s - 2) * 4)
                if c == COMBINE_AT - 1:
                    add_parts(LAST - 1, before)
                if c == COMBINE_AT:
                    combine(LAST - 1, before)
                if c == COMBINE_AT + 1:
                    mean_for_empty(LAST - 1, before)
            for s in range(SUB - 2, SUB):
                combine_bank(s, before + per_group + s * 4)
            dve.wait_ge(path_chosen, 1)
            general = dve.value_load(flag[0:1, 0:1], min_val=0, max_val=1)
            with dve.If(general != 0):
                dve.wait_ge(results_ready, GROUPS - 1 + SUB)
                nc.vector.tensor_scalar(d_logit[:], d_raw[:], b_logits[:, 1:2], None, ALU.add).then_inc(gen_d_ready, 1)
                for t in range(T):
                    last = nc.vector.scalar_tensor_tensor(out=gen_H[:, t, :], in0=H_raw[:, t, 0:D],
                                                          scalar=rstd[:, t:t + 1], in1=b_row[:],
                                                          op0=ALU.mult, op1=ALU.add)
                last.then_inc(gen_tile_free, 1)
                dve.wait_ge(gen_tile_free, 1)
                dve.wait_ge(gen_d_landed, 16)
                with dve.Fori(0, T) as s:
                    dve.wait_ge(gen_rows_landed, s * 32 + 32)
                    nc.vector.tensor_scalar(gen_score, gen_d, s_logit[:, bass.ds(s, 1)], b_att_col[:],
                                            ALU.add, ALU.add).then_inc(gen_vector_chain, 1)
                    dve.wait_ge(gen_vector_chain, s * 5 + 1)
                    nc.vector.scalar_tensor_tensor(out=gen_prob, in0=gen_adj, scalar=0.0, in1=gen_score,
                                                   op0=ALU.is_gt, op1=ALU.mult).then_inc(gen_vector_chain, 1)
                    dve.wait_ge(gen_vector_chain, s * 5 + 2)
                    nc.vector.tensor_scalar(gen_score, gen_adj, 0.0, 1.0, ALU.is_gt, ALU.subtract).then_inc(gen_vector_chain, 1)
                    dve.wait_ge(gen_vector_chain, s * 5 + 3)
                    nc.vector.scalar_tensor_tensor(out=gen_score, in0=gen_score, scalar=-NEG_INF, in1=gen_prob,
                                                   op0=ALU.mult, op1=ALU.add).then_inc(gen_vector_chain, 1)
                    dve.wait_ge(gen_vector_chain, s * 5 + 4)
                    nc.vector.tensor_reduce(gen_neg_max[:], gen_score, AX_X, ALU.max, negate=True).then_inc(gen_scores_ready, 1)
                    dve.wait_ge(gen_probs_ready, s + 1)
                    nc.vector.reciprocal(gen_inv_sum[:], gen_sum[:]).then_inc(gen_vector_chain, 1)
                    dve.wait_ge(gen_vector_chain, s * 5 + 5)
                    dve.wait_ge(gen_products, s * XP + XP)
                    nc.vector.scalar_tensor_tensor(out=gen_x[:], in0=ps_gen, scalar=gen_inv_sum[:], in1=gen_x[:],
                                                   op0=ALU.mult, op1=ALU.add).then_inc(gen_result_ready, 1)
            dve.end_ifs()

        @block.tensor
        def _(pe):
            pe.wait_ge(w_landed, 48)
            nc.tensor.matmul(ps_wa, w_T[:], a_cols[:], start=True, stop=True).then_inc(wa_in_psum, 1)
            pe.wait_ge(ident_ready, 1)
            pe.wait_ge(wa_ready, 1)
            for k in range(XP + 1):
                if k < XP:
                    if k < XP - 1:
                        pe.wait_ge(centred_ready, k + 1)
                    else:
                        pe.wait_ge(last_centred_ready, 1)
                    if k >= 2:
                        pe.wait_ge(relu_ready, k - 1)
                    for q in range(Q):
                        last = nc.tensor.transpose(ps_transposed[k % 2][:, q * P:(q + 1) * P], centred[:, k % 2, q, :], ident[:])
                    last.then_inc(transposed, 1)
                if k >= 1:
                    j = k - 1
                    pe.wait_ge(relu_ready, j + 1)
                    if j >= 2:
                        pe.wait_ge(H_ready, j - 1)
                    for q in range(Q):
                        last = nc.tensor.matmul(ps_H[j % 2][:, q // 2, (q % 2) * HE:(q % 2 + 1) * HE],
                                                relu_T[:, j % 2, q, :], w_and_wa[:], start=True, stop=True)
                    last.then_inc(H_in_psum, 1)
            pe.wait_ge(d_max_ready, 1)
            nc.tensor.transpose(ps_d_max, d_max[:], ident[:]).then_inc(d_max_row_ready, 1)
            pe.wait_ge(d_top_ready, 1)
            nc.tensor.matmul(ps_minus_D, minus_ones[:], d_top[:], start=True, stop=True).then_inc(D_in_psum, 1)
            pe.wait_ge(w_parts_ready, 1)

            def products(g, half, c):
                pe.wait_ge(masks_ready, g * CHUNKS + c + 1)
                for q in range(Q):
                    t = c * Q + q
                    starts = [t0 for t0, _ in UNITS]
                    if t in starts:
                        u = starts.index(t)
                        pe.wait_ge(quick_units, u + 1) if u < QUICK else pe.wait_ge(third_parts, u - QUICK + 1)
                    for s in range(SUB):
                        last = nc.tensor.matmul(bank[:, half * SUB + s, 0:PARTS], mask[:, c, s, q * P:(q + 1) * P],
                                                wh_rows[:, t, 0:PARTS], start=(t == 0), stop=(t == T - 1))
                last.then_inc(chunks_done, 1)

            with pe.Fori(0, GROUPS // 2 - 1) as pair:
                for c in range(CHUNKS):
                    products(pair * 2, 0, c)
                pe.wait_ge(banks_emptied, pair * (2 * SUB) + 1)
                for c in range(CHUNKS):
                    products(pair * 2 + 1, 1, c)
                pe.wait_ge(banks_emptied, pair * (2 * SUB) + SUB + 1)
            for c in range(CHUNKS):
                products(GROUPS - 2, 0, c)
            pe.wait_ge(banks_emptied, (GROUPS - 2) * SUB + 1)
            for c in range(CHUNKS):
                for s in range(SUB):
                    pe.wait_ge(masks_ready, LAST * CHUNKS + c * SUB + s + 1)
                    for q in range(Q):
                        t = c * Q + q
                        for k in range(3):
                            last = nc.tensor.matmul(bank[:, SUB + s, 0:PART], mask[:, c, s, q * P:(q + 1) * P],
                                                    wh[:, t, k, :], start=(t == 0 and k == 0),
                                                    stop=(t == T - 1 and k == 2))
                    if c == CHUNKS - 1:
                        last.then_inc(chunks_done, 1)
            pe.wait_ge(path_chosen, 1)
            general = pe.value_load(flag[0:1, 0:1], min_val=0, max_val=1)
            with pe.If(general != 0):
                with pe.Fori(0, T) as s:
                    pe.wait_ge(gen_probs_ready, s + 1)
                    pe.wait_ge(gen_tile_free, s + 1)
                    prob = gen_prob.rearrange("m (p t) -> m t p", t=T)
                    for k in range(XP + 1):
                        if k < XP:
                            if k >= 2:
                                pe.wait_ge(gen_probs_T_ready, s * XP + k - 1)
                            for q in range(Q):
                                last = nc.tensor.transpose(ps_transposed[k % 2][:, q * P:(q + 1) * P],
                                                           prob[:, k * Q + q, :], ident[:])
                            last.then_inc(gen_transposed, 1)
                        if k >= 1:
                            j = k - 1
                            pe.wait_ge(gen_probs_T_ready, s * XP + j + 1)
                            for q in range(Q):
                                last = nc.tensor.matmul(ps_gen, relu_T[:, j % 2, q, :], gen_H[:, j * Q + q, :],
                                                        start=(j == 0 and q == 0), stop=(j == XP - 1 and q == Q - 1))
                            last.then_inc(gen_products, 1)
            pe.end_ifs()


def kernel(x, adj, L0_gnn_W_fc, L0_gnn_b_fc, L0_gnn_w_att, L0_gnn_b_att):
    import numpy as np
    import concourse.bacc as bacc
    from concourse.bass_utils import run_bass_kernel_spmd

    x, adj = np.asarray(x), np.asarray(adj)
    w, b = np.asarray(L0_gnn_W_fc), np.asarray(L0_gnn_b_fc)
    a, b_att = np.asarray(L0_gnn_w_att), np.asarray(L0_gnn_b_att)
    n, d = x.shape
    tiles = n // P
    chunks = 8
    adj_t = np.ascontiguousarray(
        adj.reshape(P, tiles // SUB, SUB, P, chunks, tiles // chunks).transpose(1, 4, 3, 2, 5, 0)
    ).reshape(tiles // SUB, chunks, P, SUB, tiles // chunks * P)
    arrays = {
        "x": x, "adj_t": adj_t, "adj": adj, "w_fc": w, "w_fc_t": np.ascontiguousarray(w.T), "b_fc": b,
        "w_att": a, "a_att": np.ascontiguousarray(a.reshape(2, d).T), "b_att": b_att.reshape(1),
    }
    nc = bacc.Bacc("TRN2", target_bir_lowering=False, num_devices=1)
    ins = [nc.dram_tensor(k, v.shape, mybir.dt.from_np(v.dtype), kind="ExternalInput").ap() for k, v in arrays.items()]
    out = nc.dram_tensor("out", x.shape, mybir.dt.from_np(x.dtype), kind="ExternalOutput").ap()
    gnn_kernel(nc, *ins, out)
    return run_bass_kernel_spmd(nc, [arrays], core_ids=[0]).results[0]["out"]
```
